# Optimizing a Trainium2 kernel written in Bass

```python
import numpy as np
import jax
import jax.numpy as jnp

def _softmax(x, axis=-1):
    return jax.nn.softmax(x, axis=axis)

def _gelu(x):
    return jax.nn.gelu(x, approximate=True)

def _silu(x):
    return jax.nn.silu(x)

def _sigmoid(x):
    return jax.nn.sigmoid(x)

def _layernorm(x, axis=-1, eps=1e-05):
    m = jnp.mean(x, axis=axis, keepdims=True)
    v = jnp.var(x, axis=axis, keepdims=True)
    return (x - m) / jnp.sqrt(v + eps)

def _scatter_add(tgt, idx, src, axis=0):
    return tgt.at[idx].add(src)

def _segment_sum(src, seg, n):
    return jax.ops.segment_sum(src, seg, n)
kernel_name = 'mk_macaron_d1_jaxref_r8_d6a8ef'

def setup_inputs(seed: int=0):
    np.random.seed(seed)
    _w = jnp.asarray

    def _L0_attn_setup():
        import jax, jax.numpy as jnp
        import numpy as np
        B, S, D, H = (4, 256, 128, 16)
        HD = D // H
        LN_EPS = 1e-05
        KERN_EPS = 1e-06

        def kernel_func(q, k):
            scores = jnp.einsum('bhqd,bhkd->bhqk', q, k) / jnp.sqrt(jnp.asarray(HD, q.dtype))
            w = jax.nn.relu(scores)
            return w / (jnp.sum(w, axis=-1, keepdims=True) + KERN_EPS)
        key = jax.random.key(seed)
        k1, k2, k3 = jax.random.split(key, 3)
        scale = 1.0 / np.sqrt(D)
        return {'x': jax.random.normal(k1, (B, S, D), dtype=jnp.float32), 'w_qkv': jax.random.normal(k2, (D, 3 * D), dtype=jnp.float32) * scale, 'w_out': jax.random.normal(k3, (D, D), dtype=jnp.float32) * scale, 'b_out': jnp.zeros((D,), dtype=jnp.float32), 'gamma': jnp.ones((D,), dtype=jnp.float32), 'beta': jnp.zeros((D,), dtype=jnp.float32)}
    _L0_attn_in = _L0_attn_setup()

    def _L0_ffn_setup():
        import jax, jax.numpy as jnp
        import numpy as np
        B, S, H, F, G = (8, 256, 128, 512, 128)
        EPS = 1e-05

        def _dequant(q, scales, g):
            K, N = q.shape
            w = (q.astype(jnp.float32) - 128.0).reshape(K // g, g, N) * scales[:, None, :]
            return w.reshape(K, N)
        key = jax.random.key(seed)
        ks = jax.random.split(key, 8)
        x = jax.random.normal(ks[0], (B, S, H), dtype=jnp.float32)
        ln_gamma = jnp.ones((H,), jnp.float32)
        ln_beta = jnp.zeros((H,), jnp.float32)
        fc1_q = jax.random.randint(ks[1], (H, F), 0, 32, dtype=jnp.int32)
        fc2_q = jax.random.randint(ks[2], (F, H), 0, 32, dtype=jnp.int32)
        fc1_scales = jax.random.uniform(ks[3], (H // G, F), jnp.float32) * 0.02 + 0.001
        fc2_scales = jax.random.uniform(ks[4], (F // G, H), jnp.float32) * 0.02 + 0.001
        fc1_bias = jax.random.normal(ks[5], (F,), jnp.float32) * 0.02
        fc2_bias = jax.random.normal(ks[6], (H,), jnp.float32) * 0.02
        return {'x': x, 'ln_gamma': ln_gamma, 'ln_beta': ln_beta, 'fc1_q': fc1_q, 'fc1_scales': fc1_scales, 'fc1_bias': fc1_bias, 'fc2_q': fc2_q, 'fc2_scales': fc2_scales, 'fc2_bias': fc2_bias}
    _L0_ffn_in = _L0_ffn_setup()
    _d = {'L0_attn_x': _L0_attn_in['x'], 'L0_attn_w_qkv': _L0_attn_in['w_qkv'], 'L0_attn_w_out': _L0_attn_in['w_out'], 'L0_attn_b_out': _L0_attn_in['b_out'], 'L0_attn_gamma': _L0_attn_in['gamma'], 'L0_attn_beta': _L0_attn_in['beta'], 'L0_ffn_ln_gamma': _L0_ffn_in['ln_gamma'], 'L0_ffn_ln_beta': _L0_ffn_in['ln_beta'], 'L0_ffn_fc1_q': _L0_ffn_in['fc1_q'], 'L0_ffn_fc1_scales': _L0_ffn_in['fc1_scales'], 'L0_ffn_fc1_bias': _L0_ffn_in['fc1_bias'], 'L0_ffn_fc2_q': _L0_ffn_in['fc2_q'], 'L0_ffn_fc2_scales': _L0_ffn_in['fc2_scales'], 'L0_ffn_fc2_bias': _L0_ffn_in['fc2_bias']}
    _x0 = _d['L0_attn_x']
    _d['L0_attn_x'] = jax.random.normal(jax.random.fold_in(jax.random.key(seed), 1), (8, 512, 128), dtype=_x0.dtype)
    del _x0
    return _d

def reference(L0_attn_x, L0_attn_w_qkv, L0_attn_w_out, L0_attn_b_out, L0_attn_gamma, L0_attn_beta, L0_ffn_ln_gamma, L0_ffn_ln_beta, L0_ffn_fc1_q, L0_ffn_fc1_scales, L0_ffn_fc1_bias, L0_ffn_fc2_q, L0_ffn_fc2_scales, L0_ffn_fc2_bias):

    def _L0_attn_ref(x, w_qkv, w_out, b_out, gamma, beta):
        import jax, jax.numpy as jnp
        import numpy as np
        B, S, D, H = (4, 256, 128, 16)
        HD = D // H
        LN_EPS = 1e-05
        KERN_EPS = 1e-06

        def kernel_func(q, k):
            scores = jnp.einsum('bhqd,bhkd->bhqk', q, k) / jnp.sqrt(jnp.asarray(HD, q.dtype))
            w = jax.nn.relu(scores)
            return w / (jnp.sum(w, axis=-1, keepdims=True) + KERN_EPS)
        Bx, Sx, _ = x.shape
        qkv = (x @ w_qkv).reshape(Bx, Sx, H, 3 * HD)
        q, k, v = jnp.split(qkv, 3, axis=-1)
        q = q.transpose(0, 2, 1, 3)
        k = k.transpose(0, 2, 1, 3)
        v = v.transpose(0, 2, 1, 3)
        attn = kernel_func(q, k)
        out = jnp.einsum('bhqk,bhkd->bhqd', attn, v)
        out = out.transpose(0, 2, 1, 3).reshape(Bx, Sx, D)
        out = out @ w_out + b_out
        y = x + out
        mu = jnp.mean(y, axis=-1, keepdims=True)
        var = jnp.var(y, axis=-1, keepdims=True)
        return (y - mu) * jax.lax.rsqrt(var + LN_EPS) * gamma + beta

    def _L0_ffn_ref(x, ln_gamma, ln_beta, fc1_q, fc1_scales, fc1_bias, fc2_q, fc2_scales, fc2_bias):
        import jax, jax.numpy as jnp
        import numpy as np
        B, S, H, F, G = (8, 256, 128, 512, 128)
        EPS = 1e-05

        def _dequant(q, scales, g):
            K, N = q.shape
            w = (q.astype(jnp.float32) - 128.0).reshape(K // g, g, N) * scales[:, None, :]
            return w.reshape(K, N)
        residual = x
        mu = jnp.mean(x, axis=-1, keepdims=True)
        var = jnp.mean(jnp.square(x - mu), axis=-1, keepdims=True)
        h = (x - mu) * jax.lax.rsqrt(var + EPS) * ln_gamma + ln_beta
        hf = h.reshape(-1, H)
        w1 = _dequant(fc1_q, fc1_scales, G)
        y = hf @ w1 + fc1_bias
        y = jax.nn.silu(y)
        w2 = _dequant(fc2_q, fc2_scales, G)
        z = y @ w2 + fc2_bias
        return residual + 0.5 * z.reshape(residual.shape)
    x = L0_attn_x
    x = x + 0.5 * _L0_ffn_ref(_layernorm(x, axis=-1), L0_ffn_ln_gamma, L0_ffn_ln_beta, L0_ffn_fc1_q, L0_ffn_fc1_scales, L0_ffn_fc1_bias, L0_ffn_fc2_q, L0_ffn_fc2_scales, L0_ffn_fc2_bias)
    x = x + _L0_attn_ref(_layernorm(x, axis=-1), L0_attn_w_qkv, L0_attn_w_out, L0_attn_b_out, L0_attn_gamma, L0_attn_beta)
    x = x + 0.5 * _L0_ffn_ref(_layernorm(x, axis=-1), L0_ffn_ln_gamma, L0_ffn_ln_beta, L0_ffn_fc1_q, L0_ffn_fc1_scales, L0_ffn_fc1_bias, L0_ffn_fc2_q, L0_ffn_fc2_scales, L0_ffn_fc2_bias)
    return x

_drawn_inputs = setup_inputs


def setup_inputs(seed=0):
    import zlib

    import numpy as np

    out = dict(_drawn_inputs(seed))
    spreads = {'L0_attn_b_out': (0.0, 2.0),
     'L0_attn_gamma': (1.0, 0.6),
     'L0_attn_beta': (0.0, 0.8),
     'L0_ffn_ln_gamma': (1.0, 0.2),
     'L0_ffn_ln_beta': (0.0, 0.1)}
    factors = {'L0_ffn_fc1_bias': 29.192, 'L0_ffn_fc2_bias': 44.242}
    for name, (base, spread) in spreads.items():
        noise = np.random.default_rng([zlib.crc32(name.encode()), seed]).standard_normal(out[name].shape)
        drawn = base * np.exp(spread * noise) if base else spread * noise
        out[name] = jnp.asarray(drawn.astype(out[name].dtype))
    for name, factor in factors.items():
        out[name] = (out[name] * factor).astype(out[name].dtype)
    return out
```

```python
from contextlib import ExitStack

import concourse.bass as bass
from concourse import mybir

F32 = mybir.dt.float32
F32R = mybir.dt.float32r
BF16 = mybir.dt.bfloat16
I32 = mybir.dt.int32
ACT = mybir.ActivationFunctionType
ALU = mybir.AluOpType

P = 128
B, S, D = 8, 512, 128
H, HD = 16, 8
F = 512
TT = S // P
FT = F // P
HG = 4
NG = H // HG
STEPS = NG * TT
PARTS = 3
ROT = PARTS * HD
QK_ROWS = 96
VW = P // HG
LN_EPS = 1e-5
KERN_EPS = 1e-6
ZERO_POINT = 128.0

PRE_FILLS = ["hT", "fc1.0", "fc1.1", "fc1.2", "fc1.3", "fc2", "zT", "uT", "q", "k", "v"]
POST_FILLS = ["aT", "op", "hT", "fc1.0", "fc1.1", "fc1.2", "fc1.3", "fc2", "zT"]

SCHEDULE = [
    ([], ["o_out.3", "v_in.3"]),
    (["oT.3", "pre.x_stats"], []),
    (["post.aT"], ["pre.x_apply"]),
    (["post.op", "pre.hT"], ["pre.fc1.0", "post.y_stats"]),
    (["pre.fc1.1"], ["o_out.0", "pre.fc1.2"]),
    (["oT.0", "pre.fc1.3", "post.x2"], ["pre.fc2.0", "pre.fc2.1", "carry"]),
    (["pre.fc2.2"], ["pre.fc2.3", "post.x_apply"]),
    (["pre.zT", "pre.x1"], ["post.hT"]),
    (["post.fc1.0"], ["o_out.1", "post.fc1.1", "pre.u_apply"]),
    (["oT.1", "pre.uT"], ["post.fc1.2"]),
    (["post.fc1.3"], ["pre.q"]),
    (["pre.k"], ["pre.v", "pre.split"]),
    ([], ["o_out.2", "post.fc2.0", "post.fc2.1"]),
    (["oT.2"], ["post.fc2.2", "post.fc2.3", "v_in.0", "v_in.1"]),
    (["post.zT"], ["v_in.2"]),
    ([], []),
]


class Batch:

    def __init__(self, index, least=None):
        self.index, self.least = index, index if least is None else least

    def __add__(self, n):
        return Batch(self.index + n, self.least + n)

    def any(self, per_batch, k):
        return self.least * per_batch + k > 0

    def count(self, per_batch, k):
        assert self.any(per_batch, k), "a wait must be against a positive value"
        return self.index * per_batch + k


class Links:

    def __init__(self, per_batch):
        self.per_batch, self.k = per_batch, 0

    def start(self, batch):
        assert self.k in (0, self.per_batch), self.k
        self.batch, self.k = batch, 0

    def next(self):
        self.k += 1
        return self.batch.count(self.per_batch, self.k)


def build(nc, x, w_qkv, w_out, b_out, gamma, beta, ln_gamma, ln_beta,
          fc1_q, fc1_scales, fc1_bias, fc2_q, fc2_scales, fc2_bias, out):
    x_rows = x.rearrange("b (p t) d -> b p t d", t=TT)
    out_rows = out.rearrange("b (p t) d -> b p t d", t=TT)

    with ExitStack() as ctx:
        def sb(name, shape, dtype=F32):
            return ctx.enter_context(nc.sbuf_tensor(name, shape, dtype))

        def psum(name, shape):
            return ctx.enter_context(nc.psum_tensor(name, shape, F32))

        def sem(name):
            return ctx.enter_context(nc.semaphore(name))

        ident = sb("ident", [P, P])
        w_raw = sb("w_raw", [P, 3 * D])
        w1_raw, w2_raw = sb("w1_raw", [P, F]), sb("w2_raw", [P, FT, D])
        w1_int, w2_int = sb("w1_int", [P, F], I32), sb("w2_int", [P, FT, D], I32)
        s1_rows, s2_rows = sb("s1_rows", [P, F]), sb("s2_rows", [P, FT, D])
        w1_hi, w1_lo = sb("w1_hi", [P, F], F32R), sb("w1_lo", [P, F], F32R)
        w2_hi, w2_lo = sb("w2_hi", [P, FT, D], F32R), sb("w2_lo", [P, FT, D], F32R)
        wqk = sb("wqk", [P, 2, D])
        wqk_hi, wqk_lo = sb("wqk_hi", [P, 2, D], F32R), sb("wqk_lo", [P, 2, D], F32R)
        wv, wo = sb("wv", [P, D]), sb("wo", [P, D])
        b1_col, b2_col, b2_quarter = sb("b1_col", [P, FT]), sb("b2_col", [P, 1]), sb("b2_quarter", [P, 1])
        g_col, be_col = sb("g_col", [P, 1]), sb("be_col", [P, 1])
        gamma_rows, beta_rows, bo_rows = sb("gamma_rows", [P, D]), sb("beta_rows", [P, D]), sb("bo_rows", [P, D])

        class Stage:

            def __init__(self, n, fills):
                self.fills = fills
                self.x = sb(f"{n}_x", [P, TT, D])
                self.h = sb(f"{n}_h", [P, TT, D])
                self.u = sb(f"{n}_u", [P, TT, D])
                self.xr = sb(f"{n}_xr", [P, TT, D])
                self.t = sb(f"{n}_t", [P, S])
                self.t_hi, self.t_lo = sb(f"{n}_t_hi", [P, S], F32R), sb(f"{n}_t_lo", [P, S], F32R)
                self.y = sb(f"{n}_y", [P, 2, S])
                self.y_hi, self.y_lo = sb(f"{n}_y_hi", [P, FT, S], F32R), sb(f"{n}_y_lo", [P, FT, S], F32R)
                self.z = sb(f"{n}_z", [P, S])
                self.stats, self.mv = sb(f"{n}_stats", [P, TT, 6]), sb(f"{n}_mv", [P, TT, 2])
                self.var, self.rs, self.tmp = sb(f"{n}_var", [P, 2, TT]), sb(f"{n}_rs", [P, 2, TT]), sb(f"{n}_tmp", [P, 1])
                self.bank = psum(f"{n}_bank", [P, S])
                self.full = sem(f"{n}_bank_full")
                self.free = sem(f"{n}_bank_free")
                self.var_in = sem(f"{n}_variances")
                self.rsqrt = sem(f"{n}_rsqrt_done")
                self.rows = sem(f"{n}_rows")
                self.halves = sem(f"{n}_halves")
                self.res = sem(f"{n}_residual")
                self.t_lo_in = sem(f"{n}_t_lo_in")
                self.y_lo_in = sem(f"{n}_y_lo_in")
                self.dve_link = sem(f"{n}_dve_link")
                self.pool_link = sem(f"{n}_pool_link")

            def n(self, fill):
                return self.fills.index(fill) + 1

        pre, post = Stage("pre", PRE_FILLS), Stage("post", POST_FILLS)

        u1 = sb("u1", [P, TT, D])
        x1 = sb("x1", [P, TT, D])
        x1_beta, u1_bias = sb("x1_beta", [P, TT, D]), sb("u1_bias", [P, TT, D])
        qk = sb("qk", [P, 2, S])
        qk_parts = sb("qk_parts", [P, 2, 5, S], BF16)
        v_rows = sb("v_rows", [P, TT, D])
        q_op, k_op = sb("q_op", [QK_ROWS, H, S], BF16), sb("k_op", [QK_ROWS, H, S], BF16)
        v_op = sb("v_op", [P, TT, H, VW])
        probs = sb("probs", [P, 2, HG, S])
        o_sums = sb("o_sums", [P, 2, S])
        den, rec = sb("den", [P, TT, HG]), sb("rec", [P, TT, HG])
        a_rows = sb("a_rows", [P, TT, H, HD])
        aT = sb("aT", [P, S])
        y_rows = sb("y_rows", [P, TT, D])
        o_rows = sb("o_rows", [P, TT, D])
        scores = [psum(f"scores{i}", [P, 2, S]) for i in range(2)]
        o_bank = [psum(f"o_bank{i}", [P, S]) for i in range(2)]
        q_scratch = nc.dram_tensor("q_scratch", (PARTS, H, HD, PARTS, S), BF16, kind="Internal").ap()
        k_scratch = nc.dram_tensor("k_scratch", (H, HD, PARTS, S), BF16, kind="Internal").ap()

        minus_half, one_half = sb("minus_half", [P, 2, TT]), sb("one_half", [P, TT])

        w_loaded, w_link, w_ready = sem("w_loaded"), sem("w_link"), sem("w_ready")
        pool_ready, ident_zero = sem("pool_ready"), sem("ident_zero")
        x_loaded = sem("x_loaded")
        parts_ready = sem("parts_ready")
        scratch_in = sem("scratch_in")
        qk_in = [sem(f"qk_in{g}") for g in range(NG)]
        v_in = sem("v_in")
        scores_done = [sem(f"scores_done{i}") for i in range(2)]
        probs_done = [sem(f"probs_done{i}") for i in range(2)]
        pv_done = sem("pv_done")
        o_out = sem("o_out")
        oT_done, a_done = sem("oT_done"), sem("a_done")
        carried = sem("carried")
        x2_done = sem("x2_done")
        norm_link = sem("norm_link")
        out_ready, out_stored = sem("out_ready"), sem("out_stored")
        block = ctx.enter_context(nc.Block())

        LOADS = 13
        QK_DMAS = 2 * PARTS

        def run(engine, iteration):
            iteration(Batch(-1), core=False, has_pre=True, has_post=False)
            iteration(Batch(0), core=True, has_pre=True, has_post=False)
            with engine.Fori(1, B - 1) as b:
                iteration(Batch(b, least=1), core=True, has_pre=True, has_post=True)
            iteration(Batch(B - 1), core=True, has_pre=False, has_post=True)
            iteration(Batch(B), core=False, has_pre=False, has_post=True)

        def tasks(names, has_pre, has_post, core):
            takes = {"pre": has_pre, "post": has_post}
            for name in names:
                stage, _, rest = name.partition(".")
                if stage == "carry" or name == "v_in.3":
                    ok = core
                elif stage == "v_in":
                    ok = has_pre
                elif stage in ("o_out", "oT"):
                    ok = has_post if rest == "3" else core
                else:
                    ok = takes[stage]
                if ok:
                    yield name

        @block.sync
        def _(sp):
            for dst, src in (
                (w1_int[:, :], fc1_q), (s1_rows[:, :], fc1_scales.to_broadcast([P, F])),
                (w2_int[:, :, :], fc2_q.rearrange("(g p) n -> p g n", p=P)),
                (s2_rows[:, :, :], fc2_scales.unsqueeze(0).to_broadcast([P, FT, D])),
                (w_raw[:, :], w_qkv), (wo[:, :], w_out),
                (b1_col[:, :], fc1_bias.rearrange("(p f) -> p f", f=FT)),
            ):
                sp.dma_start(dst, src).then_inc(w_loaded, 16)

            def iteration(b, core, has_pre, has_post):
                if has_pre:
                    nb = b + 1
                    sp.wait_ge(parts_ready, nb.count(1, 1))
                    for g in range(NG):
                        if nb.any(16 * QK_DMAS, 0):
                            sp.wait_ge(qk_in[g], nb.count(16 * QK_DMAS, 0))
                    for r in range(PARTS):
                        sp.dma_start(q_scratch[r].rearrange("h d i n -> (h d) i n"),
                                     qk_parts[:, 0, r:r + PARTS, :]).then_inc(scratch_in, 16)
                    sp.dma_start(k_scratch.rearrange("h d i n -> (h d) i n"),
                                 qk_parts[:, 1, 0:PARTS, :]).then_inc(scratch_in, 16)
                    sp.wait_ge(scratch_in, nb.count(16 * (PARTS + 1), 16 * (PARTS + 1)))
                    for g in range(NG):
                        if b.any(STEPS, TT * (g + 1)):
                            sp.wait_ge(scores_done[1], b.count(STEPS, TT * (g + 1)))
                        heads = slice(HG * g, HG * (g + 1))
                        for r in range(PARTS):
                            rows = slice(ROT * r, ROT * (r + 1))
                            sp.dma_start(q_op[rows, heads, :], q_scratch[r, heads].rearrange("h d i n -> (d i) h n")
                                         ).then_inc(qk_in[g], 16)
                            sp.dma_start(k_op[rows, heads, :], k_scratch[heads].rearrange("h d i n -> (d i) h n")
                                         ).then_inc(qk_in[g], 16)

            run(sp, iteration)

        @block.tensor
        def _(pe):
            mm, transpose = nc.tensor.matmul, nc.tensor.transpose

            def next_fill(st, b, fill):
                if b.any(len(st.fills), st.n(fill) - 1 + (st is post)):
                    pe.wait_ge(st.free, b.count(len(st.fills), st.n(fill) - 1 + (st is post)))

            def transposes(st, b, fill, rows):
                for t in range(TT):
                    last = transpose(st.bank[:, P * t:P * (t + 1)], rows[:, t, :], ident[:, :])
                last.then_inc(st.full, 1)

            def three_products(bank, w_hi, w_lo, m_hi, m_lo, start, stop, low_in, low_count):
                mm(bank, w_hi, m_hi, start=start, stop=False)
                mm(bank, w_lo, m_hi, start=False, stop=False)
                pe.wait_ge(low_in, low_count)
                return mm(bank, w_hi, m_lo, start=False, stop=stop)

            def ffn(st, b, per_lo, what):
                if what == "hT":
                    pe.wait_ge(st.rows, b.count(per_lo, 1))
                    next_fill(st, b, "hT")
                    transposes(st, b, "hT", st.h)
                elif what.startswith("fc1"):
                    f = int(what[-1])
                    next_fill(st, b, what)
                    cols = slice(P * f, P * (f + 1))
                    three_products(st.bank[:, :], w1_hi[:, cols], w1_lo[:, cols], st.t_hi[:, :], st.t_lo[:, :],
                                   True, True, st.t_lo_in, b.count(per_lo, 1)
                                   ).then_inc(st.full, 1)
                elif what.startswith("fc2"):
                    f = int(what[-1])
                    if f == 0:
                        next_fill(st, b, "fc2")
                    last = three_products(st.bank[:, :], w2_hi[:, f, :], w2_lo[:, f, :],
                                          st.y_hi[:, f, :], st.y_lo[:, f, :], f == 0, f == FT - 1,
                                          st.y_lo_in, b.count(FT, f + 1))
                    if f == FT - 1:
                        last.then_inc(st.full, 1)
                elif what == "zT":
                    next_fill(st, b, "zT")
                    for t in range(TT):
                        last = transpose(st.bank[:, P * t:P * (t + 1)], st.z[:, P * t:P * (t + 1)], ident[:, :])
                    last.then_inc(st.full, 1)

            def step_scores(b, s):
                g, kt = divmod(s, TT)
                if kt == 0:
                    pe.wait_ge(qk_in[g], b.count(16 * QK_DMAS, 16 * QK_DMAS))
                for i in range(2):
                    if b.any(STEPS, s):
                        pe.wait_ge(probs_done[i], b.count(STEPS, s))
                    for j in range(2):
                        h = HG * g + 2 * i + j
                        last = mm(scores[i][:, j, :], k_op[:, h, P * kt:P * (kt + 1)], q_op[:, h, :],
                                  start=True, stop=True)
                    last.then_inc(scores_done[i], 1)

            def step_values(b, s):
                g, kt = divmod(s, TT)
                if kt == 0:
                    pe.wait_ge(v_in, b.count(NG, g + 1))
                    if b.any(NG, g - 1):
                        pe.wait_ge(a_done, b.count(NG, g - 1))
                for i in range(2):
                    if b.any(STEPS, s + 1):
                        pe.wait_ge(probs_done[i], b.count(STEPS, s + 1))
                for j in range(HG):
                    last = mm(o_bank[g % 2][VW * j:VW * (j + 1), :], v_op[:, kt, HG * g + j, :],
                              probs[:, s % 2, j, :], start=(kt == 0), stop=(kt == TT - 1))
                last.then_inc(pv_done, 1)

            def task(b, name):
                stage, _, what = name.partition(".")
                if stage == "oT":
                    g = int(what)
                    ob = b + (-1) if g == 3 else b
                    pe.wait_ge(o_out, ob.count(NG, g + 1))
                    for t in range(TT):
                        last = transpose(o_bank[g % 2][:, P * t:P * (t + 1)],
                                         o_sums[:, g % 2, P * t:P * (t + 1)], ident[:, :])
                    last.then_inc(oT_done, 1)
                elif stage == "pre":
                    nb = b + 1
                    if what == "uT":
                        pe.wait_ge(pre.rows, nb.count(2, 2))
                        next_fill(pre, nb, "uT")
                        transposes(pre, nb, "uT", u1)
                    elif what in ("q", "k"):
                        i = "qk".index(what)
                        next_fill(pre, nb, what)
                        three_products(pre.bank[:, :], wqk_hi[:, i, :], wqk_lo[:, i, :], pre.t_hi[:, :],
                                       pre.t_lo[:, :], True, True, pre.t_lo_in, nb.count(2, 2)
                                       ).then_inc(pre.full, 1)
                    elif what == "v":
                        next_fill(pre, nb, "v")
                        for t in range(TT):
                            last = mm(pre.bank[:, P * t:P * (t + 1)], pre.t[:, P * t:P * (t + 1)], wv[:, :],
                                      start=True, stop=True)
                        last.then_inc(pre.full, 1)
                    else:
                        ffn(pre, nb, 2, what)
                elif stage == "post":
                    pb = b + (-1)
                    if what == "aT":
                        if pb.any(NG, NG):
                            pe.wait_ge(a_done, pb.count(NG, NG))
                        next_fill(post, pb, "aT")
                        for t in range(TT):
                            last = transpose(post.bank[:, P * t:P * (t + 1)],
                                             a_rows[:, t, :, :].rearrange("p h d -> p (h d)"), ident[:, :])
                        last.then_inc(post.full, 1)
                    elif what == "op":
                        next_fill(post, pb, "op")
                        for t in range(TT):
                            last = mm(post.bank[:, P * t:P * (t + 1)], aT[:, P * t:P * (t + 1)], wo[:, :],
                                      start=True, stop=True)
                        last.then_inc(post.full, 1)
                    else:
                        ffn(post, pb, 1, what)

            def iteration(b, core, has_pre, has_post):
                for s, (early, late) in enumerate(SCHEDULE):
                    if core:
                        step_scores(b, s)
                    for name in tasks(early, has_pre, has_post, core):
                        task(b, name)
                    if s == 0 and has_post:
                        step_values(b + (-1), STEPS - 1)
                    elif s > 0 and core:
                        step_values(b, s - 1)
                    for name in tasks(late, has_pre, has_post, core):
                        task(b, name)

            pe.wait_ge(w_ready, 1)
            pe.wait_ge(pool_ready, 1)
            run(pe, iteration)

        @block.scalar
        def _(act):
            activation = nc.scalar.activation
            for dst, src in (
                (b2_col[:, :], fc2_bias.unsqueeze(1)), (g_col[:, :], ln_gamma.unsqueeze(1)),
                (be_col[:, :], ln_beta.unsqueeze(1)),
                (gamma_rows[:, :], gamma.unsqueeze(0).to_broadcast([P, D])),
                (beta_rows[:, :], beta.unsqueeze(0).to_broadcast([P, D])),
                (bo_rows[:, :], b_out.unsqueeze(0).to_broadcast([P, D])),
            ):
                act.dma_start(dst, src).then_inc(w_loaded, 16)

            def ffn(st, b, what):
                n, per = st.n(what if what[:3] != "fc2" else "fc2"), len(st.fills)
                free = n + (st is post)
                if what == "hT":
                    act.wait_ge(st.full, b.count(per, n))
                    activation(st.t[:, :], st.bank[:, :], ACT.Identity, bias=be_col[:, :], scale=g_col[:, :])
                    activation(st.t_hi[:, :], st.bank[:, :], ACT.Identity, bias=be_col[:, :], scale=g_col[:, :]
                               ).then_inc(st.free, 1)
                elif what.startswith("fc1"):
                    f = int(what[-1])
                    act.wait_ge(st.full, b.count(per, n))
                    if f >= 2:
                        act.wait_ge(st.y_lo_in, b.count(FT, f - 1))
                    activation(st.y[:, f % 2, :], st.bank[:, :], ACT.Silu, bias=b1_col[:, f:f + 1])
                    activation(st.y_hi[:, f, :], st.bank[:, :], ACT.Silu, bias=b1_col[:, f:f + 1]
                               ).then_inc(st.free, 1)
                elif what == "fc2.3":
                    act.wait_ge(st.full, b.count(per, n))
                    activation(st.z[:, :], st.bank[:, :], ACT.Identity, bias=b2_quarter[:, :], scale=0.25
                               ).then_inc(st.free, 1)

            def task(b, name):
                stage, _, what = name.partition(".")
                if stage == "o_out":
                    g = int(what)
                    ob = b + (-1) if g == 3 else b
                    if ob.any(STEPS, TT * (g + 1)):
                        act.wait_ge(pv_done, ob.count(STEPS, TT * (g + 1)))
                    if ob.any(NG, g - 1):
                        act.wait_ge(oT_done, ob.count(NG, g - 1))
                    activation(o_sums[:, g % 2, :], o_bank[g % 2][:, :], ACT.Copy).then_inc(o_out, 1)
                elif stage == "pre":
                    nb, per = b + 1, len(PRE_FILLS)
                    if what == "uT":
                        act.wait_ge(pre.full, nb.count(per, pre.n("uT")))
                        activation(pre.t[:, :], pre.bank[:, :], ACT.Copy)
                        activation(pre.t_hi[:, :], pre.bank[:, :], ACT.Copy).then_inc(pre.free, 1)
                    elif what in ("q", "k"):
                        i, scale = "qk".index(what), (HD ** -0.5 if what == "q" else 1.0)
                        if i == 0:
                            if nb.any(16 * (PARTS + 1), 0):
                                act.wait_ge(scratch_in, nb.count(16 * (PARTS + 1), 0))
                        act.wait_ge(pre.full, nb.count(per, pre.n(what)))
                        activation(qk[:, i, :], pre.bank[:, :], ACT.Copy, scale=scale)
                        activation(qk_parts[:, i, 0, :], pre.bank[:, :], ACT.Copy, scale=scale
                                   ).then_inc(pre.free, 1)
                    elif what == "v":
                        if nb.any(NG, 0):
                            act.wait_ge(v_in, nb.count(NG, 0))
                        act.wait_ge(pre.full, nb.count(per, pre.n("v")))
                        activation(v_rows[:, :, :], pre.bank[:, :].rearrange("p (t d) -> p t d", t=TT), ACT.Copy
                                   ).then_inc(pre.free, 1)
                    else:
                        if what in pre.fills or what == "fc2.3":
                            ffn(pre, nb, what)
                elif stage == "post":
                    pb = b + (-1)
                    if what == "aT":
                        act.wait_ge(post.full, pb.count(len(POST_FILLS), post.n("aT")))
                        activation(aT[:, :], post.bank[:, :], ACT.Copy).then_inc(post.free, 1)
                    elif what in post.fills or what == "fc2.3":
                        if what not in ("op", "zT"):
                            ffn(post, pb, what)

            def load_x(b):
                if b.any(1, 0):
                    act.wait_ge(pre.res, b.count(1, 0))
                act.dma_start(pre.x[:, :, :], x_rows[b.index]).then_inc(x_loaded, 16)

            def store_out(b):
                act.wait_ge(out_ready, b.count(1, 1))
                act.dma_start(out_rows[b.index], o_rows[:, :, :]).then_inc(out_stored, 16)

            def iteration(b, core, has_pre, has_post):
                if has_pre:
                    load_x(b + 1)
                for s, (early, late) in enumerate(SCHEDULE):
                    if core:
                        act.wait_ge(scores_done[0], b.count(STEPS, s + 1))
                        if b.any(STEPS, s - 1):
                            act.wait_ge(pv_done, b.count(STEPS, s - 1))
                        activation(probs[:, s % 2, 0:2, :], scores[0][:, :, :], ACT.Relu).then_inc(probs_done[0], 1)
                    for name in tasks(early + late, has_pre, has_post, core):
                        task(b, name)
                if has_post:
                    store_out(b + (-1))

            act.wait_ge(w_ready, 1)
            run(act, iteration)
            act.wait_ge(out_stored, 16 * (B + 1))

        @block.vector
        def _(dve):
            v = nc.vector
            pre_links = Links(7)
            post_links = Links(5)
            norm_links = Links(2 * NG)

            def prepare():
                dve.wait_ge(w_loaded, 16 * LOADS)
                v.memset(v_op[:, :, :, :], 0.0)
                v.memset(q_op[64:QK_ROWS, :, :], 0.0)
                v.memset(k_op[64:QK_ROWS, :, :], 0.0).then_inc(w_link, 1)
                dve.wait_ge(w_link, 1)
                v.memset(v_op[:, :, :, HD:HD + 1], 1.0)
                v.tensor_copy(w1_raw[:, :], w1_int[:, :])
                v.tensor_copy(w2_raw[:, :, :], w2_int[:, :, :]).then_inc(w_link, 1)
                dve.wait_ge(w_link, 2)
                v.scalar_tensor_tensor(w1_raw[:, :], w1_raw[:, :], -ZERO_POINT, s1_rows[:, :], ALU.add, ALU.mult)
                v.scalar_tensor_tensor(w2_raw[:, :, :], w2_raw[:, :, :], -ZERO_POINT,
                                                       s2_rows[:, :, :], ALU.add, ALU.mult).then_inc(w_link, 1)
                dve.wait_ge(w_link, 3)
                raw = w_raw[:, :].rearrange("p (h c d) -> p c h d", c=3, d=HD)
                for i in range(2):
                    v.tensor_copy(wqk[:, i, :].rearrange("p (h d) -> p h d", d=HD), raw[:, i])
                v.tensor_copy(wv[:, :].rearrange("p (h d) -> p h d", d=HD), raw[:, 2])
                v.tensor_scalar(b2_quarter[:, :], b2_col[:, :], 0.25, None, ALU.mult)
                v.tensor_copy(w1_hi[:, :], w1_raw[:, :])
                v.tensor_copy(w2_hi[:, :, :], w2_raw[:, :, :]).then_inc(w_link, 1)
                dve.wait_ge(w_link, 4)
                v.tensor_copy(wqk_hi[:, :, :], wqk[:, :, :]).then_inc(w_link, 1)
                dve.wait_ge(w_link, 5)
                v.tensor_tensor(w1_lo[:, :], w1_raw[:, :], w1_hi[:, :].bitcast(F32), ALU.subtract)
                v.tensor_tensor(w2_lo[:, :, :], w2_raw[:, :, :], w2_hi[:, :, :].bitcast(F32), ALU.subtract)
                v.tensor_tensor(wqk_lo[:, :, :], wqk[:, :, :], wqk_hi[:, :, :].bitcast(F32), ALU.subtract
                                ).then_inc(w_ready, 1)

            def row_stats(st, links, rows, n):
                for t in range(TT):
                    last = v.bn_stats(st.stats[:, t, :], rows[:, t, :])
                last.then_inc(st.dve_link, 1)
                dve.wait_ge(st.dve_link, links.next())
                v.tensor_copy(st.tmp[:, 0:1], st.stats[:, 0, 0:1])
                for t in range(TT):
                    last = v.bn_aggr(st.mv[:, t, :], st.stats[:, t, :])
                last.then_inc(st.dve_link, 1)
                dve.wait_ge(st.dve_link, links.next())
                var = st.mv[:, :, 1]
                last = v.tensor_scalar(st.var[:, 0, :], var, LN_EPS, None, ALU.add)
                if n == 2:
                    last = v.tensor_scalar(st.var[:, 1, :], var, 1.0 + LN_EPS, LN_EPS ** 2, ALU.mult, ALU.add)
                last.then_inc(st.var_in, 1)

            def normalise(st, dst, rows, i):
                for t in range(TT):
                    last = v.tensor_scalar(dst[:, t, :], rows[:, t, :], st.mv[:, t, 0:1], st.rs[:, i, t:t + 1],
                                           ALU.subtract, ALU.mult)
                return last

            def task(b, name):
                stage, _, what = name.partition(".")
                if stage == "oT":
                    g = int(what)
                    ob = b + (-1) if g == 3 else b
                    if g == 0:
                        norm_links.start(ob)
                        if (ob + (-1)).any(len(POST_FILLS), post.n("aT")):
                            dve.wait_ge(post.full, (ob + (-1)).count(len(POST_FILLS), post.n("aT")))
                    norm_links.batch = ob
                    dve.wait_ge(oT_done, ob.count(NG, g + 1))
                    sums = o_bank[g % 2][:, :].rearrange("p (t j c) -> p t j c", t=TT, j=HG)
                    v.tensor_scalar(den[:, :, :], sums[:, :, :, HD], KERN_EPS, None, ALU.add).then_inc(norm_link, 1)
                    dve.wait_ge(norm_link, norm_links.next())
                    v.reciprocal(rec[:, :, :], den[:, :, :]).then_inc(norm_link, 1)
                    dve.wait_ge(norm_link, norm_links.next())
                    for t in range(TT):
                        last = v.tensor_tensor(a_rows[:, t, HG * g:HG * (g + 1), :], sums[:, t, :, 0:HD],
                                               rec[:, t, :].unsqueeze(2).to_broadcast([P, HG, HD]), ALU.mult)
                    last.then_inc(a_done, 1)
                elif stage == "pre":
                    nb, per = b + 1, len(PRE_FILLS)
                    if what == "x_stats":
                        pre_links.start(nb)
                        dve.wait_ge(x_loaded, nb.count(16, 16))
                        row_stats(pre, pre_links, pre.x, 2)
                    elif what == "x_apply":
                        dve.wait_ge(pre.rsqrt, nb.count(2, 1))
                        normalise(pre, pre.h, pre.x, 1).then_inc(pre.rows, 1)
                        normalise(pre, pre.u, pre.x, 0).then_inc(pre.halves, 1)
                    elif what == "x1":
                        dve.wait_ge(pre.full, nb.count(per, pre.n("zT")))
                        dve.wait_ge(pre.res, nb.count(1, 1))
                        if nb.any(1, 0):
                            dve.wait_ge(carried, nb.count(1, 0))
                        v.tensor_tensor(x1[:, :, :], pre.bank[:, :].rearrange("p (t d) -> p t d", t=TT),
                                        pre.xr[:, :, :], ALU.add).then_inc(pre.free, 1)
                        dve.wait_ge(pre.free, nb.count(per, pre.n("zT")))
                        row_stats(pre, pre_links, x1, 1)
                    elif what == "u_apply":
                        dve.wait_ge(pre.rsqrt, nb.count(2, 2))
                        normalise(pre, u1, x1, 0).then_inc(pre.rows, 1)
                    elif what == "split":
                        dve.wait_ge(pre.free, nb.count(per, pre.n("k")))
                        v.tensor_tensor(qk[:, :, :], qk[:, :, :], qk_parts[:, :, 0, :],
                                                            ALU.subtract).then_inc(pre.dve_link, 1)
                        dve.wait_ge(pre.dve_link, pre_links.next())
                        v.tensor_copy(qk_parts[:, :, 1, :], qk[:, :, :]).then_inc(pre.dve_link, 1)
                        dve.wait_ge(pre.dve_link, pre_links.next())
                        v.tensor_copy(qk_parts[:, 0, 3:5, :], qk_parts[:, 0, 0:2, :])
                        v.tensor_tensor(qk_parts[:, :, 2, :], qk[:, :, :],
                                                            qk_parts[:, :, 1, :], ALU.subtract).then_inc(pre.dve_link, 1)
                        dve.wait_ge(pre.dve_link, pre_links.next())
                        v.tensor_copy(pre.tmp[:, :], pre.mv[:, 0, 0:1]).then_inc(parts_ready, 1)
                elif stage == "post":
                    pb, per = b + (-1), len(POST_FILLS)
                    if what == "y_stats":
                        post_links.start(pb)
                        if pb.any(per, post.n("op")):
                            dve.wait_ge(post.full, pb.count(per, post.n("op")))
                        if pb.any(1, 1):
                            dve.wait_ge(carried, pb.count(1, 1))
                        v.tensor_tensor(y_rows[:, :, :], post.bank[:, :].rearrange("p (t d) -> p t d", t=TT),
                                        u1_bias[:, :, :], ALU.add).then_inc(post.free, 1)
                        dve.wait_ge(post.free, pb.count(per, post.n("op") + 1))
                        row_stats(post, post_links, y_rows, 1)
                    elif what == "x2":
                        dve.wait_ge(post.rsqrt, pb.count(2, 1))
                        for t in range(TT):
                            last = v.scalar_tensor_tensor(y_rows[:, t, :], y_rows[:, t, :], post.mv[:, t, 0:1],
                                                          gamma_rows[:, :], ALU.subtract, ALU.mult)
                        last.then_inc(post.dve_link, 1)
                        dve.wait_ge(post.dve_link, post_links.next())
                        for t in range(TT):
                            last = v.scalar_tensor_tensor(post.x[:, t, :], y_rows[:, t, :], post.rs[:, 0, t:t + 1],
                                                          x1_beta[:, t, :], ALU.mult, ALU.add)
                        last.then_inc(x2_done, 1)
                        dve.wait_ge(x2_done, pb.count(1, 1))
                        row_stats(post, post_links, post.x, 2)
                    elif what == "x_apply":
                        dve.wait_ge(post.rsqrt, pb.count(2, 2))
                        normalise(post, post.h, post.x, 1).then_inc(post.rows, 1)
                        normalise(post, post.u, post.x, 0).then_inc(post.halves, 1)
                    elif what == "zT":
                        if pb.any(per, post.n("zT")):
                            dve.wait_ge(post.full, pb.count(per, post.n("zT")))
                        dve.wait_ge(post.res, pb.count(1, 1))
                        dve.wait_ge(out_stored, pb.count(16, 16))
                        v.tensor_tensor(o_rows[:, :, :], post.bank[:, :].rearrange("p (t d) -> p t d", t=TT),
                                        post.xr[:, :, :], ALU.add).then_inc(post.free, 1)
                        dve.wait_ge(post.free, pb.count(per, post.n("zT") + 1))
                        v.tensor_copy(post.tmp[:, :], post.mv[:, 0, 0:1]).then_inc(out_ready, 1)

            def iteration(b, core, has_pre, has_post):
                for s, (early, late) in enumerate(SCHEDULE):
                    if core:
                        dve.wait_ge(scores_done[1], b.count(STEPS, s + 1))
                        if b.any(STEPS, s - 1):
                            dve.wait_ge(pv_done, b.count(STEPS, s - 1))
                        v.tensor_scalar(probs[:, s % 2, 2:4, :], scores[1][:, :, :], 0.0, None, ALU.max
                                        ).then_inc(probs_done[1], 1)
                    for name in tasks(early + late, has_pre, has_post, core):
                        task(b, name)

            v.memset(rec[:, 0, 0:1], 0.0).then_inc(post.free, 1)
            v.memset(den[:, 0, 0:1], 0.0).then_inc(out_stored, 16)
            prepare()
            run(dve, iteration)

        @block.gpsimd
        def _(pool):
            p = nc.gpsimd
            p.memset(minus_half[:, :, :], -0.5)
            p.memset(one_half[:, :], 0.5).then_inc(ident_zero, 1)
            p.memset(ident[:, :], 0.0).then_inc(ident_zero, 1)
            pool.wait_ge(ident_zero, 2)
            p.affine_select(out=ident[:, :], in_=ident[:, :], compare_op=ALU.not_equal, fill=1.0, base=0,
                            pattern=[[-1, P]], channel_multiplier=1).then_inc(pool_ready, 1)
            pre_links = Links(1)
            post_links = Links(1)

            def deviations(st, links, b, k, n):
                pool.wait_ge(st.var_in, b.count(2, k))
                last = p.tensor_tensor(st.rs[:, 0:n, :], st.var[:, 0:n, :], minus_half[:, 0:n, :], ALU.pow)
                if n == 2:
                    last.then_inc(st.pool_link, 1)
                    pool.wait_ge(st.pool_link, links.next())
                    last = p.tensor_tensor(st.rs[:, 0, :], st.rs[:, 0, :], one_half[:, :], ALU.mult)
                last.then_inc(st.rsqrt, 1)

            def residual(st, b):
                pool.wait_ge(st.halves, b.count(1, 1))
                p.tensor_tensor(st.xr[:, :, :], st.u[:, :, :], st.x[:, :, :], ALU.add
                                       ).then_inc(st.res, 1)

            def low_t(st, b, fill):
                pool.wait_ge(st.free, b.count(len(st.fills), st.n(fill) + (st is post)))
                p.tensor_tensor(st.t_lo[:, :], st.t[:, :], st.t_hi[:, :].bitcast(F32), ALU.subtract
                                ).then_inc(st.t_lo_in, 1)

            def low_y(st, b, what):
                f = int(what[-1])
                pool.wait_ge(st.free, b.count(len(st.fills), st.n(what) + (st is post)))
                p.tensor_tensor(st.y_lo[:, f, :], st.y[:, f % 2, :], st.y_hi[:, f, :].bitcast(F32), ALU.subtract
                                ).then_inc(st.y_lo_in, 1)

            def task(b, name):
                stage, _, what = name.partition(".")
                if stage == "v_in":
                    g = int(what)
                    vb = b if g == 3 else b + 1
                    pool.wait_ge(pre.free, vb.count(len(PRE_FILLS), pre.n("v")))
                    if (vb + (-1)).any(STEPS, TT * (g + 1)):
                        pool.wait_ge(pv_done, (vb + (-1)).count(STEPS, TT * (g + 1)))
                    heads = slice(HG * g, HG * (g + 1))
                    rows = v_rows[:, :, :].rearrange("p t (h d) -> p t h d", d=HD)[:, :, heads, :]
                    ones = v_op[:, :, heads, HD:HD + 1].to_broadcast([P, TT, HG, HD])
                    p.tensor_tensor(v_op[:, :, heads, 0:HD], rows, ones, ALU.mult).then_inc(v_in, 1)
                elif stage == "carry":
                    pool.wait_ge(pre.rows, b.count(2, 2))
                    if b.any(1, 0):
                        pool.wait_ge(x2_done, b.count(1, 0))
                    rows = lambda r: r[:, :].unsqueeze(1).to_broadcast([P, TT, D])
                    p.tensor_tensor(x1_beta[:, :, :], x1[:, :, :], rows(beta_rows), ALU.add)
                    p.tensor_tensor(u1_bias[:, :, :], u1[:, :, :], rows(bo_rows), ALU.add).then_inc(carried, 1)
                elif stage == "pre":
                    nb = b + 1
                    if what == "x_stats":
                        pre_links.start(nb)
                        deviations(pre, pre_links, nb, 1, 2)
                    elif what == "x_apply":
                        residual(pre, nb)
                    elif what in ("hT", "uT"):
                        low_t(pre, nb, what)
                    elif what.startswith("fc1"):
                        low_y(pre, nb, what)
                    elif what == "x1":
                        deviations(pre, pre_links, nb, 2, 1)
                elif stage == "post":
                    pb = b + (-1)
                    if what == "y_stats":
                        post_links.start(pb)
                        deviations(post, post_links, pb, 1, 1)
                    elif what == "x2":
                        deviations(post, post_links, pb, 2, 2)
                    elif what == "x_apply":
                        residual(post, pb)
                    elif what == "hT":
                        low_t(post, pb, what)
                    elif what.startswith("fc1"):
                        low_y(post, pb, what)

            def iteration(b, core, has_pre, has_post):
                for early, late in SCHEDULE:
                    for name in tasks(early + late, has_pre, has_post, core):
                        task(b, name)

            pool.wait_ge(w_ready, 1)
            run(pool, iteration)


_INS = ['L0_attn_x', 'L0_attn_w_qkv', 'L0_attn_w_out', 'L0_attn_b_out', 'L0_attn_gamma', 'L0_attn_beta',
        'L0_ffn_ln_gamma', 'L0_ffn_ln_beta', 'L0_ffn_fc1_q', 'L0_ffn_fc1_scales', 'L0_ffn_fc1_bias',
        'L0_ffn_fc2_q', 'L0_ffn_fc2_scales', 'L0_ffn_fc2_bias']


def kernel(**inputs):
    import numpy as _np
    import concourse.bacc as _bacc
    from concourse import mybir as _mybir
    from concourse.bass_utils import run_bass_kernel_spmd as _run

    nc = _bacc.Bacc("TRN2", target_bir_lowering=False, num_devices=1)
    arrays, args = {}, []
    for name in _INS:
        a = _np.ascontiguousarray(inputs[name])
        if name == 'L0_ffn_fc1_bias':
            a = _np.ascontiguousarray(a.reshape(FT, P).T).reshape(-1)
        arrays[f"in_{name}_dram"] = a
        args.append(nc.dram_tensor(f"in_{name}_dram", a.shape, _mybir.dt.from_np(a.dtype), kind="ExternalInput").ap())
    out = nc.dram_tensor("out_0_dram", (B, S, D), F32, kind="ExternalOutput").ap()
    build(nc, *args, out)
    r = _run(nc, [arrays], core_ids=[0])
    return r.results[0]["out_0_dram"]
```

```python
from contextlib import ExitStack

import concourse.bass as bass
from concourse import mybir

F32 = mybir.dt.float32
F32R = mybir.dt.float32r
BF16 = mybir.dt.bfloat16
I32 = mybir.dt.int32
ACT = mybir.ActivationFunctionType
ALU = mybir.AluOpType

P = 128
B, S, D = 8, 512, 128
H, HD = 16, 8
F = 512
TT = S // P
FT = F // P
HG = 4
NG = H // HG
STEPS = NG * TT
PARTS = 3
ROT = PARTS * HD
QK_ROWS = 96
VW = P // HG
LN_EPS = 1e-5
KERN_EPS = 1e-6
ZERO_POINT = 128.0

PRE_FILLS = ["hT", "fc1.0", "fc1.1", "fc1.2", "fc1.3", "fc2", "zT", "uT", "q", "k", "v"]
POST_FILLS = ["aT", "op", "hT", "fc1.0", "fc1.1", "fc1.2", "fc1.3", "fc2", "zT"]

SCHEDULE = [
    ([], ["o_out.3", "v_in.3", "hold", "pre.fc2.0"]),
    (["oT.3", "pre.fc2.1"], ["pre.fc2.2"]),
    (["pre.fc2.3"], ["post.aT"]),
    (["pre.zT", "pre.x1"], ["post.op", "post.y_stats"]),
    ([], ["o_out.0", "carry_u", "pre.u_apply", "post.x2", "carry"]),
    (["oT.0", "pre.uT"], []),
    (["pre.q"], ["post.x_apply"]),
    (["pre.k"], ["post.hT", "pre.split"]),
    (["pre.v"], ["o_out.1", "post.fc1.0", "pre.x_stats"]),
    (["oT.1"], ["post.fc1.1", "pre.x_apply"]),
    (["pre.hT"], ["post.fc1.2"]),
    (["pre.fc1.0"], ["post.fc1.3", "v_in.0", "v_in.1"]),
    (["pre.fc1.1"], ["o_out.2", "post.fc2.0", "post.fc2.1"]),
    (["oT.2", "pre.fc1.2"], ["post.fc2.2", "v_in.2"]),
    (["pre.fc1.3"], ["post.fc2.3"]),
    ([], ["post.zT"]),
]
PRE_FIRST = ["x_stats", "x_apply", "hT", "fc1.0", "fc1.1", "fc1.2", "fc1.3"]


def batch_offset(stage, what):
    if stage == "pre":
        return 2 if what in PRE_FIRST else 1
    if stage == "post":
        return -1
    if stage in ("o_out", "oT"):
        return -1 if what == "3" else 0
    if stage == "v_in":
        return 0 if what == "3" else 1
    return 0


class Batch:

    def __init__(self, index, least=None):
        self.index, self.least = index, index if least is None else least

    def __add__(self, n):
        return Batch(self.index + n, self.least + n)

    def exists(self):
        return not isinstance(self.index, int) or 0 <= self.index < B

    def any(self, per_batch, k):
        return self.least * per_batch + k > 0

    def count(self, per_batch, k):
        assert self.any(per_batch, k), "a wait must be against a positive value"
        return self.index * per_batch + k


def tasks(b, names):
    for name in names:
        stage, _, what = name.partition(".")
        batch = b + batch_offset(stage, what)
        if batch.exists():
            yield stage, what, batch


def build(nc, x, w_qkv, w_out, b_out, gamma, beta, ln_gamma, ln_beta,
          fc1_q, fc1_scales, fc1_bias, fc2_q, fc2_scales, fc2_bias, out):
    x_rows = x.rearrange("b (p t) d -> b p t d", t=TT)
    out_rows = out.rearrange("b (p t) d -> b p t d", t=TT)

    with ExitStack() as ctx:
        def sb(name, shape, dtype=F32):
            return ctx.enter_context(nc.sbuf_tensor(name, shape, dtype))

        def psum(name, shape):
            return ctx.enter_context(nc.psum_tensor(name, shape, F32))

        def sem(name):
            return ctx.enter_context(nc.semaphore(name))

        ident = sb("ident", [P, P])
        w_raw = sb("w_raw", [P, 3 * D])
        w1_raw, w2_raw = sb("w1_raw", [P, F]), sb("w2_raw", [P, FT, D])
        w1_int, w2_int = sb("w1_int", [P, F], I32), sb("w2_int", [P, FT, D], I32)
        s1_rows, s2_rows = sb("s1_rows", [P, F]), sb("s2_rows", [P, FT, D])
        w1_hi, w1_lo = sb("w1_hi", [P, F], F32R), sb("w1_lo", [P, F], F32R)
        w2_hi, w2_lo = sb("w2_hi", [P, FT, D], F32R), sb("w2_lo", [P, FT, D], F32R)
        wqk = sb("wqk", [P, 2, D])
        wqk_hi, wqk_lo = sb("wqk_hi", [P, 2, D], F32R), sb("wqk_lo", [P, 2, D], F32R)
        wv, wo = sb("wv", [P, D]), sb("wo", [P, D])
        b1_col, b2_col, b2_quarter = sb("b1_col", [P, FT]), sb("b2_col", [P, 1]), sb("b2_quarter", [P, 1])
        g_col, be_col = sb("g_col", [P, 1]), sb("be_col", [P, 1])
        gamma_rows, beta_rows, bo_rows = sb("gamma_rows", [P, D]), sb("beta_rows", [P, D]), sb("bo_rows", [P, D])

        class Stage:

            def __init__(self, n, fills):
                self.fills = fills
                self.x = sb(f"{n}_x", [P, TT, D])
                self.h = sb(f"{n}_h", [P, TT, D])
                self.u = sb(f"{n}_u", [P, TT, D])
                self.xr = sb(f"{n}_xr", [P, TT, D])
                self.t = sb(f"{n}_t", [P, S])
                self.t_hi, self.t_lo = sb(f"{n}_t_hi", [P, S], F32R), sb(f"{n}_t_lo", [P, S], F32R)
                self.y = sb(f"{n}_y", [P, 2, S])
                self.y_hi, self.y_lo = sb(f"{n}_y_hi", [P, FT, S], F32R), sb(f"{n}_y_lo", [P, FT, S], F32R)
                self.z = sb(f"{n}_z", [P, S])
                self.stats, self.mv = sb(f"{n}_stats", [P, TT, 6]), sb(f"{n}_mv", [P, TT, 2])
                self.var, self.rs, self.tmp = sb(f"{n}_var", [P, 2, TT]), sb(f"{n}_rs", [P, 2, TT]), sb(f"{n}_tmp", [P, 1])
                self.bank = psum(f"{n}_bank", [P, S])
                self.full = sem(f"{n}_bank_full")
                self.free = sem(f"{n}_bank_free")
                self.var_in = sem(f"{n}_variances")
                self.rsqrt = sem(f"{n}_rsqrt_done")
                self.rows = sem(f"{n}_rows")
                self.halves = sem(f"{n}_halves")
                self.res = sem(f"{n}_residual")
                self.t_lo_in = sem(f"{n}_t_lo_in")
                self.y_lo_in = sem(f"{n}_y_lo_in")
                self.dve_link = sem(f"{n}_dve_link")
                self.pool_link = sem(f"{n}_pool_link")

            def n(self, fill):
                return self.fills.index(fill) + 1

        pre, post = Stage("pre", PRE_FILLS), Stage("post", POST_FILLS)

        u1 = sb("u1", [P, TT, D])
        x1 = sb("x1", [P, TT, D])
        x1_held, x1_beta = sb("x1_held", [P, TT, D]), sb("x1_beta", [P, TT, D])
        u1_bias = sb("u1_bias", [P, TT, D])
        qk = sb("qk", [P, 2, S])
        qk_parts = sb("qk_parts", [P, 2, 5, S], BF16)
        v_rows = sb("v_rows", [P, TT, D])
        q_op, k_op = sb("q_op", [QK_ROWS, H, S], BF16), sb("k_op", [QK_ROWS, H, S], BF16)
        v_op = sb("v_op", [P, TT, H, VW])
        probs = sb("probs", [P, 2, HG, S])
        o_sums = sb("o_sums", [P, 2, S])
        den, rec = sb("den", [P, TT, HG]), sb("rec", [P, TT, HG])
        a_rows = sb("a_rows", [P, TT, H, HD])
        aT = sb("aT", [P, S])
        y_rows = sb("y_rows", [P, TT, D])
        o_rows = sb("o_rows", [P, TT, D])
        scores = [psum(f"scores{i}", [P, 2, S]) for i in range(2)]
        o_bank = [psum(f"o_bank{i}", [P, S]) for i in range(2)]
        q_scratch = nc.dram_tensor("q_scratch", (PARTS, H, HD, PARTS, S), BF16, kind="Internal").ap()
        k_scratch = nc.dram_tensor("k_scratch", (H, HD, PARTS, S), BF16, kind="Internal").ap()

        minus_half, one_half = sb("minus_half", [P, 2, TT]), sb("one_half", [P, TT])

        w1_loaded, w2_loaded, wqkv_loaded, wo_loaded = sem("w1_loaded"), sem("w2_loaded"), sem("wqkv_loaded"), sem("wo_loaded")
        columns_loaded, b2_loaded, rows_loaded = sem("columns_loaded"), sem("b2_loaded"), sem("rows_loaded")
        w_link = sem("w_link")
        w1_ready, w2_ready, wqkv_ready = sem("w1_ready"), sem("w2_ready"), sem("wqkv_ready")
        zero_rows, v_ready = sem("zero_rows"), sem("v_ready")
        split_link = sem("split_link")
        held, u_carried = sem("held"), sem("u_carried")
        pool_ready, ident_zero = sem("pool_ready"), sem("ident_zero")
        x_loaded = sem("x_loaded")
        parts_ready = sem("parts_ready")
        scratch_in = sem("scratch_in")
        qk_in = [sem(f"qk_in{g}") for g in range(NG)]
        v_in = sem("v_in")
        scores_done = [sem(f"scores_done{i}") for i in range(2)]
        probs_done = [sem(f"probs_done{i}") for i in range(2)]
        pv_done = sem("pv_done")
        o_out = sem("o_out")
        oT_done, a_done = sem("oT_done"), sem("a_done")
        carried = sem("carried")
        x2_done = sem("x2_done")
        norm_link = sem("norm_link")
        out_stored = sem("out_stored")
        block = ctx.enter_context(nc.Block())

        QK_DMAS = 2 * PARTS

        def run(engine, iteration):
            for b in (-2, -1, 0):
                iteration(Batch(b))
            with engine.Fori(1, B - 2) as b:
                iteration(Batch(b, least=1))
            for b in (B - 2, B - 1, B):
                iteration(Batch(b))

        @block.sync
        def _(sp):
            for dst, src, loaded in (
                (w1_int[:, :], fc1_q, w1_loaded), (s1_rows[:, :], fc1_scales.to_broadcast([P, F]), w1_loaded),
                (w2_int[:, :, :], fc2_q.rearrange("(g p) n -> p g n", p=P), w2_loaded),
                (s2_rows[:, :, :], fc2_scales.unsqueeze(0).to_broadcast([P, FT, D]), w2_loaded),
                (w_raw[:, :], w_qkv, wqkv_loaded), (wo[:, :], w_out, wo_loaded),
            ):
                sp.dma_start(dst, src).then_inc(loaded, 16)

            def iteration(b):
                nb = b + 1
                if nb.exists():
                    sp.wait_ge(parts_ready, nb.count(1, 1))
                    for g in range(NG):
                        if nb.any(16 * QK_DMAS, 0):
                            sp.wait_ge(qk_in[g], nb.count(16 * QK_DMAS, 0))
                    for r in range(PARTS):
                        sp.dma_start(q_scratch[r].rearrange("h d i n -> (h d) i n"),
                                     qk_parts[:, 0, r:r + PARTS, :]).then_inc(scratch_in, 16)
                    sp.dma_start(k_scratch.rearrange("h d i n -> (h d) i n"),
                                 qk_parts[:, 1, 0:PARTS, :]).then_inc(scratch_in, 16)
                    sp.wait_ge(scratch_in, nb.count(16 * (PARTS + 1), 16 * (PARTS + 1)))
                    if nb.least == 0:
                        sp.wait_ge(zero_rows, 1)
                    for g in range(NG):
                        if b.any(STEPS, TT * (g + 1)):
                            sp.wait_ge(scores_done[1], b.count(STEPS, TT * (g + 1)))
                        heads = slice(HG * g, HG * (g + 1))
                        for r in range(PARTS):
                            rows = slice(ROT * r, ROT * (r + 1))
                            sp.dma_start(q_op[rows, heads, :], q_scratch[r, heads].rearrange("h d i n -> (d i) h n")
                                         ).then_inc(qk_in[g], 16)
                            sp.dma_start(k_op[rows, heads, :], k_scratch[heads].rearrange("h d i n -> (d i) h n")
                                         ).then_inc(qk_in[g], 16)

            run(sp, iteration)

        @block.tensor
        def _(pe):
            mm, transpose = nc.tensor.matmul, nc.tensor.transpose

            def next_fill(st, b, fill):
                if b.any(len(st.fills), st.n(fill) - 1 + (st is post)):
                    pe.wait_ge(st.free, b.count(len(st.fills), st.n(fill) - 1 + (st is post)))

            def transposes(st, b, fill, rows):
                for t in range(TT):
                    last = transpose(st.bank[:, P * t:P * (t + 1)], rows[:, t, :], ident[:, :])
                last.then_inc(st.full, 1)

            def three_products(bank, w_hi, w_lo, m_hi, m_lo, start, stop, low_in, low_count):
                mm(bank, w_hi, m_hi, start=start, stop=False)
                mm(bank, w_lo, m_hi, start=False, stop=False)
                pe.wait_ge(low_in, low_count)
                return mm(bank, w_hi, m_lo, start=False, stop=stop)

            def ffn(st, b, per_lo, what):
                if what == "hT":
                    pe.wait_ge(st.rows, b.count(per_lo, 1))
                    next_fill(st, b, "hT")
                    transposes(st, b, "hT", st.h)
                elif what.startswith("fc1"):
                    f = int(what[-1])
                    if st is pre and b.least == 0:
                        pe.wait_ge(w1_ready, 1)
                    next_fill(st, b, what)
                    cols = slice(P * f, P * (f + 1))
                    three_products(st.bank[:, :], w1_hi[:, cols], w1_lo[:, cols], st.t_hi[:, :], st.t_lo[:, :],
                                   True, True, st.t_lo_in, b.count(per_lo, 1)
                                   ).then_inc(st.full, 1)
                elif what.startswith("fc2"):
                    f = int(what[-1])
                    if st is pre and b.least == 0:
                        pe.wait_ge(w2_ready, 1)
                    if f == 0:
                        next_fill(st, b, "fc2")
                    last = three_products(st.bank[:, :], w2_hi[:, f, :], w2_lo[:, f, :],
                                          st.y_hi[:, f, :], st.y_lo[:, f, :], f == 0, f == FT - 1,
                                          st.y_lo_in, b.count(FT, f + 1))
                    if f == FT - 1:
                        last.then_inc(st.full, 1)
                elif what == "zT":
                    next_fill(st, b, "zT")
                    for t in range(TT):
                        last = transpose(st.bank[:, P * t:P * (t + 1)], st.z[:, P * t:P * (t + 1)], ident[:, :])
                    last.then_inc(st.full, 1)

            def step_scores(b, s):
                g, kt = divmod(s, TT)
                if kt == 0:
                    pe.wait_ge(qk_in[g], b.count(16 * QK_DMAS, 16 * QK_DMAS))
                for i in range(2):
                    if b.any(STEPS, s):
                        pe.wait_ge(probs_done[i], b.count(STEPS, s))
                    for j in range(2):
                        h = HG * g + 2 * i + j
                        last = mm(scores[i][:, j, :], k_op[:, h, P * kt:P * (kt + 1)], q_op[:, h, :],
                                  start=True, stop=True)
                    last.then_inc(scores_done[i], 1)

            def step_values(b, s):
                g, kt = divmod(s, TT)
                if kt == 0:
                    pe.wait_ge(v_in, b.count(NG, g + 1))
                    if b.any(NG, g - 1):
                        pe.wait_ge(a_done, b.count(NG, g - 1))
                for i in range(2):
                    if b.any(STEPS, s + 1):
                        pe.wait_ge(probs_done[i], b.count(STEPS, s + 1))
                for j in range(HG):
                    last = mm(o_bank[g % 2][VW * j:VW * (j + 1), :], v_op[:, kt, HG * g + j, :],
                              probs[:, s % 2, j, :], start=(kt == 0), stop=(kt == TT - 1))
                last.then_inc(pv_done, 1)

            def task(stage, what, b):
                if stage == "oT":
                    g = int(what)
                    pe.wait_ge(o_out, b.count(NG, g + 1))
                    for t in range(TT):
                        last = transpose(o_bank[g % 2][:, P * t:P * (t + 1)],
                                         o_sums[:, g % 2, P * t:P * (t + 1)], ident[:, :])
                    last.then_inc(oT_done, 1)
                elif stage == "pre":
                    if what == "uT":
                        pe.wait_ge(pre.rows, b.count(2, 2))
                        next_fill(pre, b, "uT")
                        transposes(pre, b, "uT", u1)
                    elif what in ("q", "k"):
                        i = "qk".index(what)
                        if b.least == 0:
                            pe.wait_ge(wqkv_ready, 1)
                        next_fill(pre, b, what)
                        three_products(pre.bank[:, :], wqk_hi[:, i, :], wqk_lo[:, i, :], pre.t_hi[:, :],
                                       pre.t_lo[:, :], True, True, pre.t_lo_in, b.count(2, 2)
                                       ).then_inc(pre.full, 1)
                    elif what == "v":
                        next_fill(pre, b, "v")
                        for t in range(TT):
                            last = mm(pre.bank[:, P * t:P * (t + 1)], pre.t[:, P * t:P * (t + 1)], wv[:, :],
                                      start=True, stop=True)
                        last.then_inc(pre.full, 1)
                    else:
                        ffn(pre, b, 2, what)
                elif stage == "post":
                    if what == "aT":
                        pe.wait_ge(a_done, b.count(NG, NG))
                        next_fill(post, b, "aT")
                        for t in range(TT):
                            last = transpose(post.bank[:, P * t:P * (t + 1)],
                                             a_rows[:, t, :, :].rearrange("p h d -> p (h d)"), ident[:, :])
                        last.then_inc(post.full, 1)
                    elif what == "op":
                        if b.least == 0:
                            pe.wait_ge(wo_loaded, 16)
                        next_fill(post, b, "op")
                        for t in range(TT):
                            last = mm(post.bank[:, P * t:P * (t + 1)], aT[:, P * t:P * (t + 1)], wo[:, :],
                                      start=True, stop=True)
                        last.then_inc(post.full, 1)
                    else:
                        ffn(post, b, 1, what)

            def iteration(b):
                for s, (early, late) in enumerate(SCHEDULE):
                    if b.exists():
                        step_scores(b, s)
                    for stage, what, tb in tasks(b, early):
                        task(stage, what, tb)
                    if s == 0 and (b + (-1)).exists():
                        step_values(b + (-1), STEPS - 1)
                    elif s > 0 and b.exists():
                        step_values(b, s - 1)
                    for stage, what, tb in tasks(b, late):
                        task(stage, what, tb)

            pe.wait_ge(pool_ready, 1)
            run(pe, iteration)

        @block.scalar
        def _(act):
            activation = nc.scalar.activation
            act.dma_start(pre.x[:, :, :], x_rows[0]).then_inc(x_loaded, 16)
            for dst, src, loaded in (
                (g_col[:, :], ln_gamma.unsqueeze(1), columns_loaded), (be_col[:, :], ln_beta.unsqueeze(1), columns_loaded),
                (b1_col[:, :], fc1_bias.rearrange("(p f) -> p f", f=FT), columns_loaded),
                (b2_col[:, :], fc2_bias.unsqueeze(1), b2_loaded),
                (gamma_rows[:, :], gamma.unsqueeze(0).to_broadcast([P, D]), rows_loaded),
                (beta_rows[:, :], beta.unsqueeze(0).to_broadcast([P, D]), rows_loaded),
                (bo_rows[:, :], b_out.unsqueeze(0).to_broadcast([P, D]), rows_loaded),
            ):
                act.dma_start(dst, src).then_inc(loaded, 16)

            def ffn(st, b, what):
                n, per = st.n(what if what[:3] != "fc2" else "fc2"), len(st.fills)
                free = n + (st is post)
                if what == "hT":
                    act.wait_ge(st.full, b.count(per, n))
                    activation(st.t[:, :], st.bank[:, :], ACT.Identity, bias=be_col[:, :], scale=g_col[:, :])
                    activation(st.t_hi[:, :], st.bank[:, :], ACT.Identity, bias=be_col[:, :], scale=g_col[:, :]
                               ).then_inc(st.free, 1)
                elif what.startswith("fc1"):
                    f = int(what[-1])
                    act.wait_ge(st.full, b.count(per, n))
                    if f >= 2:
                        act.wait_ge(st.y_lo_in, b.count(FT, f - 1))
                    activation(st.y[:, f % 2, :], st.bank[:, :], ACT.Silu, bias=b1_col[:, f:f + 1])
                    activation(st.y_hi[:, f, :], st.bank[:, :], ACT.Silu, bias=b1_col[:, f:f + 1]
                               ).then_inc(st.free, 1)
                elif what == "fc2.3":
                    if st is pre and b.least == 0:
                        act.wait_ge(w2_ready, 1)
                    act.wait_ge(st.full, b.count(per, n))
                    activation(st.z[:, :], st.bank[:, :], ACT.Identity, bias=b2_quarter[:, :], scale=0.25
                               ).then_inc(st.free, 1)

            def task(stage, what, b):
                if stage == "o_out":
                    g = int(what)
                    act.wait_ge(pv_done, b.count(STEPS, TT * (g + 1)))
                    if b.any(NG, g - 1):
                        act.wait_ge(oT_done, b.count(NG, g - 1))
                    activation(o_sums[:, g % 2, :], o_bank[g % 2][:, :], ACT.Copy).then_inc(o_out, 1)
                elif stage == "pre":
                    per = len(PRE_FILLS)
                    if what == "uT":
                        act.wait_ge(pre.full, b.count(per, pre.n("uT")))
                        activation(pre.t[:, :], pre.bank[:, :], ACT.Copy)
                        activation(pre.t_hi[:, :], pre.bank[:, :], ACT.Copy).then_inc(pre.free, 1)
                    elif what in ("q", "k"):
                        i, scale = "qk".index(what), (HD ** -0.5 if what == "q" else 1.0)
                        if i == 0:
                            if b.any(16 * (PARTS + 1), 0):
                                act.wait_ge(scratch_in, b.count(16 * (PARTS + 1), 0))
                        act.wait_ge(pre.full, b.count(per, pre.n(what)))
                        activation(qk[:, i, :], pre.bank[:, :], ACT.Copy, scale=scale)
                        activation(qk_parts[:, i, 0, :], pre.bank[:, :], ACT.Copy, scale=scale
                                   ).then_inc(pre.free, 1)
                    elif what == "v":
                        if b.any(NG, 0):
                            act.wait_ge(v_in, b.count(NG, 0))
                        act.wait_ge(pre.full, b.count(per, pre.n("v")))
                        activation(v_rows[:, :, :], pre.bank[:, :].rearrange("p (t d) -> p t d", t=TT), ACT.Copy
                                   ).then_inc(pre.free, 1)
                    else:
                        if what in pre.fills or what == "fc2.3":
                            ffn(pre, b, what)
                elif stage == "post":
                    if what == "aT":
                        act.wait_ge(post.full, b.count(len(POST_FILLS), post.n("aT")))
                        activation(aT[:, :], post.bank[:, :], ACT.Copy).then_inc(post.free, 1)
                    elif what in post.fills or what == "fc2.3":
                        if what not in ("op", "zT"):
                            ffn(post, b, what)
                elif stage == "carry":
                    act.wait_ge(held, b.count(1, 1))
                    if b.any(1, 0):
                        act.wait_ge(x2_done, b.count(1, 0))
                    activation(x1_beta[:, :, :], x1_held[:, :, :], ACT.Copy).then_inc(carried, 1)

            def load_x(b):
                if b.any(1, 0):
                    act.wait_ge(pre.res, b.count(1, 0))
                act.dma_start(pre.x[:, :, :], x_rows[b.index]).then_inc(x_loaded, 16)

            def store_out(b):
                act.wait_ge(post.free, b.count(len(POST_FILLS), post.n("zT") + 1))
                act.dma_start(out_rows[b.index], o_rows[:, :, :]).then_inc(out_stored, 16)

            def iteration(b):
                if b.least > -2 and (b + 2).exists():
                    load_x(b + 2)
                for s, (early, late) in enumerate(SCHEDULE):
                    if b.exists():
                        act.wait_ge(scores_done[0], b.count(STEPS, s + 1))
                        if b.any(STEPS, s - 1):
                            act.wait_ge(pv_done, b.count(STEPS, s - 1))
                        activation(probs[:, s % 2, 0:2, :], scores[0][:, :, :], ACT.Relu).then_inc(probs_done[0], 1)
                    for stage, what, tb in tasks(b, early + late):
                        task(stage, what, tb)
                if (b + (-1)).exists():
                    store_out(b + (-1))

            act.wait_ge(columns_loaded, 48)
            run(act, iteration)
            act.wait_ge(out_stored, 16 * (B + 1))

        @block.vector
        def _(dve):
            v = nc.vector
            PRE_LINKS, POST_LINKS, SPLIT_LINKS, NORM_LINKS = 4, 5, 2, 2 * NG

            def prepare():
                dve.wait_ge(w1_loaded, 32)
                v.tensor_copy(w1_raw[:, :], w1_int[:, :]).then_inc(w_link, 1)
                dve.wait_ge(w2_loaded, 32)
                v.tensor_copy(w2_raw[:, :, :], w2_int[:, :, :]).then_inc(w_link, 1)
                dve.wait_ge(w_link, 2)
                v.scalar_tensor_tensor(w1_raw[:, :], w1_raw[:, :], -ZERO_POINT, s1_rows[:, :],
                                       ALU.add, ALU.mult).then_inc(w_link, 1)
                v.scalar_tensor_tensor(w2_raw[:, :, :], w2_raw[:, :, :], -ZERO_POINT, s2_rows[:, :, :],
                                       ALU.add, ALU.mult).then_inc(w_link, 1)
                dve.wait_ge(w_link, 4)
                v.tensor_copy(w1_hi[:, :], w1_raw[:, :]).then_inc(w_link, 1)
                v.tensor_copy(w2_hi[:, :, :], w2_raw[:, :, :]).then_inc(w_link, 1)
                dve.wait_ge(w_link, 6)
                v.tensor_tensor(w1_lo[:, :], w1_raw[:, :], w1_hi[:, :].bitcast(F32), ALU.subtract).then_inc(w1_ready, 1)
                dve.wait_ge(b2_loaded, 16)
                v.tensor_scalar(b2_quarter[:, :], b2_col[:, :], 0.25, None, ALU.mult)
                v.tensor_tensor(w2_lo[:, :, :], w2_raw[:, :, :], w2_hi[:, :, :].bitcast(F32), ALU.subtract
                                ).then_inc(w2_ready, 1)
                dve.wait_ge(wqkv_loaded, 16)
                raw = w_raw[:, :].rearrange("p (h c d) -> p c h d", c=3, d=HD)
                for i in range(2):
                    v.tensor_copy(wqk[:, i, :].rearrange("p (h d) -> p h d", d=HD), raw[:, i])
                v.tensor_copy(wv[:, :].rearrange("p (h d) -> p h d", d=HD), raw[:, 2]).then_inc(w_link, 1)
                dve.wait_ge(w_link, 7)
                v.tensor_copy(wqk_hi[:, :, :], wqk[:, :, :]).then_inc(w_link, 1)
                dve.wait_ge(w_link, 8)
                v.tensor_tensor(wqk_lo[:, :, :], wqk[:, :, :], wqk_hi[:, :, :].bitcast(F32), ALU.subtract
                                ).then_inc(wqkv_ready, 1)
                v.memset(q_op[64:QK_ROWS, :, :].bitcast(F32), 0.0)
                v.memset(k_op[64:QK_ROWS, :, :].bitcast(F32), 0.0).then_inc(zero_rows, 1)

            def row_stats(st, b, per, k, rows, n):
                for t in range(TT):
                    last = v.bn_stats(st.stats[:, t, :], rows[:, t, :])
                last.then_inc(st.dve_link, 1)
                dve.wait_ge(st.dve_link, b.count(per, k + 1))
                v.tensor_copy(st.tmp[:, 0:1], st.stats[:, 0, 0:1])
                for t in range(TT):
                    last = v.bn_aggr(st.mv[:, t, :], st.stats[:, t, :])
                last.then_inc(st.dve_link, 1)
                dve.wait_ge(st.dve_link, b.count(per, k + 2))
                var = st.mv[:, :, 1]
                last = v.tensor_scalar(st.var[:, 0, :], var, LN_EPS, None, ALU.add)
                if n == 2:
                    last = v.tensor_scalar(st.var[:, 1, :], var, 1.0 + LN_EPS, LN_EPS ** 2, ALU.mult, ALU.add)
                last.then_inc(st.var_in, 1)

            def normalise(st, dst, rows, i):
                for t in range(TT):
                    last = v.tensor_scalar(dst[:, t, :], rows[:, t, :], st.mv[:, t, 0:1], st.rs[:, i, t:t + 1],
                                           ALU.subtract, ALU.mult)
                return last

            def task(stage, what, b):
                if stage == "oT":
                    g = int(what)
                    if g == 0:
                        if (b + (-1)).any(len(POST_FILLS), post.n("aT")):
                            dve.wait_ge(post.full, (b + (-1)).count(len(POST_FILLS), post.n("aT")))
                    dve.wait_ge(oT_done, b.count(NG, g + 1))
                    sums = o_bank[g % 2][:, :].rearrange("p (t j c) -> p t j c", t=TT, j=HG)
                    v.tensor_scalar(den[:, :, :], sums[:, :, :, HD], KERN_EPS, None, ALU.add).then_inc(norm_link, 1)
                    dve.wait_ge(norm_link, b.count(NORM_LINKS, 2 * g + 1))
                    v.reciprocal(rec[:, :, :], den[:, :, :]).then_inc(norm_link, 1)
                    dve.wait_ge(norm_link, b.count(NORM_LINKS, 2 * g + 2))
                    for t in range(TT):
                        last = v.tensor_tensor(a_rows[:, t, HG * g:HG * (g + 1), :], sums[:, t, :, 0:HD],
                                               rec[:, t, :].unsqueeze(2).to_broadcast([P, HG, HD]), ALU.mult)
                    last.then_inc(a_done, 1)
                elif stage == "pre":
                    per = len(PRE_FILLS)
                    if what == "x_stats":
                        dve.wait_ge(x_loaded, b.count(16, 16))
                        row_stats(pre, b, PRE_LINKS, 0, pre.x, 2)
                    elif what == "x_apply":
                        dve.wait_ge(pre.rsqrt, b.count(2, 1))
                        normalise(pre, pre.h, pre.x, 1).then_inc(pre.rows, 1)
                        normalise(pre, pre.u, pre.x, 0).then_inc(pre.halves, 1)
                    elif what == "x1":
                        dve.wait_ge(pre.full, b.count(per, pre.n("zT")))
                        dve.wait_ge(pre.res, b.count(1, 1))
                        if b.any(1, 0):
                            dve.wait_ge(held, b.count(1, 0))
                        v.tensor_tensor(x1[:, :, :], pre.bank[:, :].rearrange("p (t d) -> p t d", t=TT),
                                        pre.xr[:, :, :], ALU.add).then_inc(pre.free, 1)
                        dve.wait_ge(pre.free, b.count(per, pre.n("zT")))
                        row_stats(pre, b, PRE_LINKS, 2, x1, 1)
                    elif what == "u_apply":
                        dve.wait_ge(pre.rsqrt, b.count(2, 2))
                        if b.any(1, 0):
                            dve.wait_ge(u_carried, b.count(1, 0))
                        normalise(pre, u1, x1, 0).then_inc(pre.rows, 1)
                    elif what == "split":
                        dve.wait_ge(pre.free, b.count(per, pre.n("k")))
                        v.tensor_tensor(qk[:, :, :], qk[:, :, :], qk_parts[:, :, 0, :], ALU.subtract
                                        ).then_inc(split_link, 1)
                        dve.wait_ge(split_link, b.count(SPLIT_LINKS, 1))
                        v.tensor_copy(qk_parts[:, :, 1, :], qk[:, :, :]).then_inc(split_link, 1)
                        dve.wait_ge(split_link, b.count(SPLIT_LINKS, 2))
                        v.tensor_copy(qk_parts[:, 0, 3:5, :], qk_parts[:, 0, 0:2, :])
                        v.tensor_tensor(qk_parts[:, :, 2, :], qk[:, :, :], qk_parts[:, :, 1, :], ALU.subtract
                                        ).then_inc(parts_ready, 1)
                elif stage == "post":
                    per = len(POST_FILLS)
                    if what == "y_stats":
                        dve.wait_ge(post.full, b.count(per, post.n("op")))
                        dve.wait_ge(u_carried, b.count(1, 1))
                        v.tensor_tensor(y_rows[:, :, :], post.bank[:, :].rearrange("p (t d) -> p t d", t=TT),
                                        u1_bias[:, :, :], ALU.add).then_inc(post.free, 1)
                        dve.wait_ge(post.free, b.count(per, post.n("op") + 1))
                        row_stats(post, b, POST_LINKS, 0, y_rows, 1)
                    elif what == "x2":
                        dve.wait_ge(post.rsqrt, b.count(2, 1))
                        dve.wait_ge(carried, b.count(1, 1))
                        for t in range(TT):
                            last = v.scalar_tensor_tensor(y_rows[:, t, :], y_rows[:, t, :], post.mv[:, t, 0:1],
                                                          gamma_rows[:, :], ALU.subtract, ALU.mult)
                        last.then_inc(post.dve_link, 1)
                        dve.wait_ge(post.dve_link, b.count(POST_LINKS, 3))
                        for t in range(TT):
                            last = v.scalar_tensor_tensor(post.x[:, t, :], y_rows[:, t, :], post.rs[:, 0, t:t + 1],
                                                          x1_beta[:, t, :], ALU.mult, ALU.add)
                        last.then_inc(x2_done, 1)
                        dve.wait_ge(x2_done, b.count(1, 1))
                        row_stats(post, b, POST_LINKS, 3, post.x, 2)
                    elif what == "x_apply":
                        dve.wait_ge(post.rsqrt, b.count(2, 2))
                        normalise(post, post.h, post.x, 1).then_inc(post.rows, 1)
                        normalise(post, post.u, post.x, 0).then_inc(post.halves, 1)
                    elif what == "zT":
                        dve.wait_ge(post.full, b.count(per, post.n("zT")))
                        dve.wait_ge(post.res, b.count(1, 1))
                        dve.wait_ge(out_stored, b.count(16, 16))
                        v.tensor_tensor(o_rows[:, :, :], post.bank[:, :].rearrange("p (t d) -> p t d", t=TT),
                                        post.xr[:, :, :], ALU.add).then_inc(post.free, 1)

            def iteration(b):
                for s, (early, late) in enumerate(SCHEDULE):
                    if b.exists():
                        dve.wait_ge(scores_done[1], b.count(STEPS, s + 1))
                        if b.any(STEPS, s - 1):
                            dve.wait_ge(pv_done, b.count(STEPS, s - 1))
                        v.tensor_scalar(probs[:, s % 2, 2:4, :], scores[1][:, :, :], 0.0, None, ALU.max
                                        ).then_inc(probs_done[1], 1)
                    for stage, what, tb in tasks(b, early + late):
                        task(stage, what, tb)
                if b.least == -2:
                    prepare()

            v.memset(rec[:, 0, 0:1], 0.0).then_inc(post.free, 1)
            v.memset(den[:, 0, 0:1], 0.0).then_inc(out_stored, 16)
            run(dve, iteration)

        @block.gpsimd
        def _(pool):
            p = nc.gpsimd
            p.memset(minus_half[:, :, :], -0.5)
            p.memset(one_half[:, :], 0.5).then_inc(ident_zero, 1)
            p.memset(ident[:, :], 0.0).then_inc(ident_zero, 1)
            pool.wait_ge(ident_zero, 2)
            p.affine_select(out=ident[:, :], in_=ident[:, :], compare_op=ALU.not_equal, fill=1.0, base=0,
                            pattern=[[-1, P]], channel_multiplier=1).then_inc(pool_ready, 1)
            p.memset(v_op[:, :, :, :], 0.0).then_inc(v_ready, 1)
            pool.wait_ge(v_ready, 1)
            p.memset(v_op[:, :, :, HD:HD + 1], 1.0).then_inc(v_ready, 1)

            def deviations(st, b, k, n):
                pool.wait_ge(st.var_in, b.count(2, k))
                last = p.tensor_tensor(st.rs[:, 0:n, :], st.var[:, 0:n, :], minus_half[:, 0:n, :], ALU.pow)
                if n == 2:
                    last.then_inc(st.pool_link, 1)
                    pool.wait_ge(st.pool_link, b.count(1, 1))
                    last = p.tensor_tensor(st.rs[:, 0, :], st.rs[:, 0, :], one_half[:, :], ALU.mult)
                last.then_inc(st.rsqrt, 1)

            def residual(st, b):
                pool.wait_ge(st.halves, b.count(1, 1))
                p.tensor_tensor(st.xr[:, :, :], st.u[:, :, :], st.x[:, :, :], ALU.add
                                       ).then_inc(st.res, 1)

            def low_t(st, b, fill):
                pool.wait_ge(st.free, b.count(len(st.fills), st.n(fill) + (st is post)))
                p.tensor_tensor(st.t_lo[:, :], st.t[:, :], st.t_hi[:, :].bitcast(F32), ALU.subtract
                                ).then_inc(st.t_lo_in, 1)

            def low_y(st, b, what):
                f = int(what[-1])
                pool.wait_ge(st.free, b.count(len(st.fills), st.n(what) + (st is post)))
                p.tensor_tensor(st.y_lo[:, f, :], st.y[:, f % 2, :], st.y_hi[:, f, :].bitcast(F32), ALU.subtract
                                ).then_inc(st.y_lo_in, 1)

            def task(stage, what, b):
                if stage == "v_in":
                    g = int(what)
                    if b.least == 0:
                        pool.wait_ge(v_ready, 2)
                    pool.wait_ge(pre.free, b.count(len(PRE_FILLS), pre.n("v")))
                    if (b + (-1)).any(STEPS, TT * (g + 1)):
                        pool.wait_ge(pv_done, (b + (-1)).count(STEPS, TT * (g + 1)))
                    heads = slice(HG * g, HG * (g + 1))
                    rows = v_rows[:, :, :].rearrange("p t (h d) -> p t h d", d=HD)[:, :, heads, :]
                    ones = v_op[:, :, heads, HD:HD + 1].to_broadcast([P, TT, HG, HD])
                    p.tensor_tensor(v_op[:, :, heads, 0:HD], rows, ones, ALU.mult).then_inc(v_in, 1)
                elif stage == "hold":
                    pool.wait_ge(pre.rows, b.count(2, 2))
                    if b.least == 0:
                        pool.wait_ge(rows_loaded, 48)
                    if b.any(1, 0):
                        pool.wait_ge(carried, b.count(1, 0))
                    p.tensor_tensor(x1_held[:, :, :], x1[:, :, :], beta_rows[:, :].unsqueeze(1).to_broadcast([P, TT, D]),
                                    ALU.add).then_inc(held, 1)
                elif stage == "carry_u":
                    last_batch, per = b + (-1), len(POST_FILLS)
                    if last_batch.any(per, post.n("op") + 1):
                        pool.wait_ge(post.free, last_batch.count(per, post.n("op") + 1))
                    p.tensor_tensor(u1_bias[:, :, :], u1[:, :, :], bo_rows[:, :].unsqueeze(1).to_broadcast([P, TT, D]),
                                    ALU.add).then_inc(u_carried, 1)
                elif stage == "pre":
                    if what == "x_stats":
                        deviations(pre, b, 1, 2)
                    elif what == "x_apply":
                        residual(pre, b)
                    elif what in ("hT", "uT"):
                        low_t(pre, b, what)
                    elif what.startswith("fc1"):
                        low_y(pre, b, what)
                    elif what == "x1":
                        deviations(pre, b, 2, 1)
                elif stage == "post":
                    if what == "y_stats":
                        deviations(post, b, 1, 1)
                    elif what == "x2":
                        deviations(post, b, 2, 2)
                    elif what == "x_apply":
                        residual(post, b)
                    elif what == "hT":
                        low_t(post, b, what)
                    elif what.startswith("fc1"):
                        low_y(post, b, what)

            def iteration(b):
                for early, late in SCHEDULE:
                    for stage, what, tb in tasks(b, early + late):
                        task(stage, what, tb)

            run(pool, iteration)


_INS = ['L0_attn_x', 'L0_attn_w_qkv', 'L0_attn_w_out', 'L0_attn_b_out', 'L0_attn_gamma', 'L0_attn_beta',
        'L0_ffn_ln_gamma', 'L0_ffn_ln_beta', 'L0_ffn_fc1_q', 'L0_ffn_fc1_scales', 'L0_ffn_fc1_bias',
        'L0_ffn_fc2_q', 'L0_ffn_fc2_scales', 'L0_ffn_fc2_bias']


def kernel(**inputs):
    import numpy as _np
    import concourse.bacc as _bacc
    from concourse import mybir as _mybir
    from concourse.bass_utils import run_bass_kernel_spmd as _run

    nc = _bacc.Bacc("TRN2", target_bir_lowering=False, num_devices=1)
    arrays, args = {}, []
    for name in _INS:
        a = _np.ascontiguousarray(inputs[name])
        if name == 'L0_ffn_fc1_bias':
            a = _np.ascontiguousarray(a.reshape(FT, P).T).reshape(-1)
        arrays[f"in_{name}_dram"] = a
        args.append(nc.dram_tensor(f"in_{name}_dram", a.shape, _mybir.dt.from_np(a.dtype), kind="ExternalInput").ap())
    out = nc.dram_tensor("out_0_dram", (B, S, D), F32, kind="ExternalOutput").ap()
    build(nc, *args, out)
    r = _run(nc, [arrays], core_ids=[0])
    return r.results[0]["out_0_dram"]
```

```python
from contextlib import ExitStack

import concourse.bass as bass
from concourse import mybir

F32 = mybir.dt.float32
F32R = mybir.dt.float32r
BF16 = mybir.dt.bfloat16
I32 = mybir.dt.int32
ACT = mybir.ActivationFunctionType
ALU = mybir.AluOpType

P = 128
B, S, D = 8, 512, 128
H, HD = 16, 8
F = 512
TT = S // P
FT = F // P
HG = 4
NG = H // HG
NP, PH = NG // 2, 2 * HG
STEPS = NG * TT
PARTS = 3
ROT = PARTS * HD
QK_ROWS = 96
VW = P // HG
HW = VW // 2
LN_EPS = 1e-5
KERN_EPS = 1e-6
ZERO_POINT = 128.0

PRE_FILLS = ["hT", "fc1.0", "fc1.1", "fc1.2", "fc1.3", "fc2", "zT", "uT", "q", "k", "v"]
POST_FILLS = ["aT", "op", "hT", "fc1.0", "fc1.1", "fc1.2", "fc1.3", "fc2", "zT"]

SCHEDULE = [
    ([], ["o_out.1", "v_in.3", "hold", "pre.fc1.1", "pre.high.1", "pre.low.1"]),
    (["pre.fc1.2", "pre.high.2", "pre.low.2", "oT.1"], ["pre.fc1.3", "pre.high.3", "pre.low.3"]),
    ([], ["post.aT", "pre.fc2.0"]),
    (["pre.xr"], ["pre.fc2.1"]),
    (["post.op", "post.y"], ["post.y_stats"]),
    (["carry_u", "pre.fc2.2", "pre.load_x"], ["post.y_gamma", "pre.fc2.3"]),
    (["post.x2"], []),
    (["pre.zT", "post.x2_stats"], ["pre.x1"]),
    (["pre.x1_stats", "o_out.0", "post.x_apply"], []),
    ([], ["post.hT", "pre.u_apply", "carry"]),
    ([], ["oT.0", "pre.uT"]),
    (["post.fc1.0", "post.high.0", "post.low.0"], ["pre.q"]),
    (["pre.split_q", "post.fc1.1", "post.high.1", "post.low.1"],
     ["pre.k", "pre.x_stats", "post.fc1.2", "post.high.2", "post.low.2", "post.xr"]),
    ([], ["pre.v", "pre.split_k", "post.fc1.3", "post.high.3", "post.low.3", "v_in.0", "v_in.1", "pre.x_apply"]),
    (["post.fc2.0"], ["post.fc2.1", "post.fc2.2", "v_in.2", "pre.hT", "post.fc2.3"]),
    ([], ["post.zT", "pre.fc1.0", "pre.high.0", "pre.low.0"]),
]
PRE_FIRST = ["load_x", "x_stats", "x_apply", "hT", "fc1.0", "high.0", "low.0"]


def heads_of(g):
    return slice(PH * (g // 2) + g % 2, PH * (g // 2 + 1), 2)


def batch_offset(stage, what):
    if stage == "pre":
        return 2 if what in PRE_FIRST else 1
    if stage == "post":
        return -1
    if stage in ("o_out", "oT"):
        return -1 if what == "1" else 0
    if stage == "v_in":
        return 0 if what == "3" else 1
    return 0


class Batch:

    def __init__(self, index, least=None):
        self.index, self.least = index, index if least is None else least

    def __add__(self, n):
        return Batch(self.index + n, self.least + n)

    def exists(self):
        return not isinstance(self.index, int) or 0 <= self.index < B

    def any(self, per_batch, k):
        return self.least * per_batch + k > 0

    def count(self, per_batch, k):
        assert self.any(per_batch, k), "a wait must be against a positive value"
        return self.index * per_batch + k


def tasks(b, names):
    for name in names:
        stage, _, what = name.partition(".")
        batch = b + batch_offset(stage, what)
        if batch.exists():
            yield stage, what, batch


def build(nc, x, w_qkv, w_out, b_out, gamma, beta, ln_gamma, ln_beta,
          fc1_q, fc1_scales, fc1_bias, fc2_q, fc2_scales, fc2_bias, out):
    x_rows = x.rearrange("b (p t) d -> b p t d", t=TT)
    out_rows = out.rearrange("b (p t) d -> b p t d", t=TT)

    with ExitStack() as ctx:
        def sb(name, shape, dtype=F32):
            return ctx.enter_context(nc.sbuf_tensor(name, shape, dtype))

        def psum(name, shape):
            return ctx.enter_context(nc.psum_tensor(name, shape, F32))

        def sem(name):
            return ctx.enter_context(nc.semaphore(name))

        ident = sb("ident", [P, P])
        w_raw = sb("w_raw", [P, 3 * D])
        w1_raw, w2_raw = sb("w1_raw", [P, F]), sb("w2_raw", [P, FT, D])
        w1_int, w2_int = sb("w1_int", [P, F], I32), sb("w2_int", [P, FT, D], I32)
        s1_rows, s2_rows = sb("s1_rows", [P, F]), sb("s2_rows", [P, FT, D])
        w1_hi, w1_lo = sb("w1_hi", [P, F], F32R), sb("w1_lo", [P, F], F32R)
        w2_hi, w2_lo = sb("w2_hi", [P, FT, D], F32R), sb("w2_lo", [P, FT, D], F32R)
        wqk = sb("wqk", [P, 2, D])
        wqk_hi, wqk_lo = sb("wqk_hi", [P, 2, D], F32R), sb("wqk_lo", [P, 2, D], F32R)
        wv, wo = sb("wv", [P, D]), sb("wo", [P, D])
        b1_col, b2_col, b2_quarter = sb("b1_col", [P, FT]), sb("b2_col", [P, 1]), sb("b2_quarter", [P, 1])
        g_col, be_col = sb("g_col", [P, 1]), sb("be_col", [P, 1])
        gamma_rows, beta_rows, bo_rows = sb("gamma_rows", [P, D]), sb("beta_rows", [P, D]), sb("bo_rows", [P, D])

        class Stage:

            def __init__(self, n, fills):
                self.fills = fills
                self.x = sb(f"{n}_x", [P, TT, D])
                self.h = sb(f"{n}_h", [P, TT, D])
                self.xr = sb(f"{n}_xr", [P, TT, D])
                self.t = sb(f"{n}_t", [P, S])
                self.t_hi, self.t_lo = sb(f"{n}_t_hi", [P, S], F32R), sb(f"{n}_t_lo", [P, S], F32R)
                self.y = sb(f"{n}_y", [P, 2, S])
                self.y_hi, self.y_lo = sb(f"{n}_y_hi", [P, FT, S], F32R), sb(f"{n}_y_lo", [P, FT, S], F32R)
                self.z = sb(f"{n}_z", [P, S])
                self.stats, self.mv = sb(f"{n}_stats", [P, TT, 6]), sb(f"{n}_mv", [P, TT, 2])
                self.var, self.rs, self.tmp = sb(f"{n}_var", [P, 2, TT]), sb(f"{n}_rs", [P, 2, TT]), sb(f"{n}_tmp", [P, 1])
                self.bank = psum(f"{n}_bank", [P, S])
                self.full = sem(f"{n}_bank_full")
                self.free = sem(f"{n}_bank_free")
                self.var_in = sem(f"{n}_variances")
                self.rsqrt = sem(f"{n}_rsqrt_done")
                self.rows = sem(f"{n}_rows")
                self.minus_mean, self.minus_mr = sb(f"{n}_minus_mean", [P, TT]), sb(f"{n}_minus_mr", [P, TT])
                self.half_r, self.mix = sb(f"{n}_half_r", [P, TT]), sb(f"{n}_mix", [P, 2, TT])
                self.centred = sem(f"{n}_centred")
                self.mixed = sem(f"{n}_mixed")
                self.res = sem(f"{n}_residual")
                self.t_lo_in = sem(f"{n}_t_lo_in")
                self.y_hi_in = sem(f"{n}_y_hi_in")
                self.y_lo_in = sem(f"{n}_y_lo_in")
                self.dve_link = sem(f"{n}_dve_link")
                self.pool_link = sem(f"{n}_pool_link")

            def n(self, fill):
                return self.fills.index(fill) + 1

        pre, post = Stage("pre", PRE_FILLS), Stage("post", POST_FILLS)

        def alone(st, b):
            return isinstance(b.index, int) and b.index == (0 if st is pre else B - 1)

        def fc1_bank(st, b, f):
            return (post if st is pre else pre).bank if alone(st, b) and f % 2 == 1 else st.bank

        u1 = sb("u1", [P, TT, D])
        x1 = sb("x1", [P, TT, D])
        x1_held, x1_beta = sb("x1_held", [P, TT, D]), sb("x1_beta", [P, TT, D])
        u1_bias = sb("u1_bias", [P, TT, D])
        qk = sb("qk", [P, 2, S])
        qk_parts = sb("qk_parts", [P, 2, PARTS, S], BF16)
        v_rows = sb("v_rows", [P, TT, D])
        q_op, k_op = sb("q_op", [QK_ROWS, H, S], BF16), sb("k_op", [QK_ROWS, H, S], BF16)
        v_op = sb("v_op", [P, TT, H, VW])
        probs = sb("probs", [P, 2, HG, S])
        o_sums = sb("o_sums", [P, 2, S])
        den, rec = sb("den", [P, TT, PH]), sb("rec", [P, TT, PH])
        a_rows = sb("a_rows", [P, TT, H, HD])
        aT = sb("aT", [P, S])
        y_rows = sb("y_rows", [P, TT, D])
        o_rows = sb("o_rows", [P, TT, D])
        scores = [psum(f"scores{i}", [P, 2, S]) for i in range(2)]
        o_bank = [psum(f"o_bank{i}", [P, S]) for i in range(2)]
        q_scratch = nc.dram_tensor("q_scratch", (H, 2 * PARTS - 1, HD, S), BF16, kind="Internal").ap()
        k_scratch = nc.dram_tensor("k_scratch", (H, PARTS, HD, S), BF16, kind="Internal").ap()

        minus_half, half, ones = sb("minus_half", [P, TT]), sb("half", [P, TT]), sb("ones", [P, TT])

        w1_loaded, w2_loaded = sem("w1_loaded"), sem("w2_loaded")
        wqkv_loaded, wo_loaded = sem("wqkv_loaded"), sem("wo_loaded")
        columns_loaded, b2_loaded, rows_loaded = sem("columns_loaded"), sem("b2_loaded"), sem("rows_loaded")
        w_link = sem("w_link")
        w1_ready, w2_ready, wqkv_ready = sem("w1_ready"), sem("w2_ready"), sem("wqkv_ready")
        zero_rows, v_ready = sem("zero_rows"), sem("v_ready")
        split_link = sem("split_link")
        held, u_carried = sem("held"), sem("u_carried")
        pool_ready, ident_zero = sem("pool_ready"), sem("ident_zero")
        x_loaded = sem("x_loaded")
        high_in = [sem("q_high_in"), sem("k_high_in")]
        parts_ready = [sem("q_parts_ready"), sem("k_parts_ready")]
        q_scratch_in, k_scratch_in = sem("q_scratch_in"), sem("k_scratch_in")
        qk_in = [sem(f"qk_in{g}") for g in range(NG)]
        v_in = sem("v_in")
        scores_done = [sem(f"scores_done{i}") for i in range(2)]
        probs_done = [sem(f"probs_done{i}") for i in range(2)]
        pv_done = sem("pv_done")
        o_out = sem("o_out")
        oT_done, a_done = sem("oT_done"), sem("a_done")
        carried = sem("carried")
        x2_done = sem("x2_done")
        norm_link = sem("norm_link")
        out_stored = sem("out_stored")
        block = ctx.enter_context(nc.Block())

        QK_DMAS = 2 * PARTS
        Q_DMAS = 2 * PARTS - 1

        def run(engine, iteration):
            for b in (-2, -1, 0):
                iteration(Batch(b))
            with engine.Fori(1, B - 2) as b:
                iteration(Batch(b, least=1))
            for b in (B - 2, B - 1, B):
                iteration(Batch(b))

        @block.sync
        def _(sp):
            for dst, src, loaded in (
                (w1_int[:, :], fc1_q, w1_loaded), (s1_rows[:, :], fc1_scales.to_broadcast([P, F]), w1_loaded),
                (w2_int[:, :, :], fc2_q.rearrange("(g p) n -> p g n", p=P), w2_loaded),
                (s2_rows[:, :, :], fc2_scales.unsqueeze(0).to_broadcast([P, FT, D]), w2_loaded),
                (w_raw[:, :], w_qkv, wqkv_loaded), (wo[:, :], w_out, wo_loaded),
            ):
                sp.dma_start(dst, src).then_inc(loaded, 16)

            def iteration(b):
                nb = b + 1
                if nb.exists():
                    sp.wait_ge(parts_ready[0], nb.count(1, 1))
                    for g in range(NG):
                        if nb.any(16 * QK_DMAS, 0):
                            sp.wait_ge(qk_in[g], nb.count(16 * QK_DMAS, 0))
                    for i in range(2 * PARTS - 1):
                        sp.dma_start(q_scratch[:, i], qk_parts[:, 0, i % PARTS, :]).then_inc(q_scratch_in, 16)
                    sp.wait_ge(parts_ready[1], nb.count(1, 1))
                    for i in range(PARTS):
                        sp.dma_start(k_scratch[:, i], qk_parts[:, 1, i, :]).then_inc(k_scratch_in, 16)
                    if nb.least == 0:
                        sp.wait_ge(zero_rows, 1)
                    for g in range(NG):
                        if b.any(STEPS, TT * (g + 1)):
                            sp.wait_ge(scores_done[1], b.count(2 * STEPS, 2 * TT * (g + 1)))
                        heads = heads_of(g)
                        if g == 0:
                            sp.wait_ge(q_scratch_in, nb.count(16 * Q_DMAS, 16 * Q_DMAS))
                        for r in range(PARTS):
                            sp.dma_start(q_op[ROT * r:ROT * (r + 1), heads, :],
                                         q_scratch[heads, r:r + PARTS].rearrange("h i d n -> (i d) h n")
                                         ).then_inc(qk_in[g], 16)
                        if g == 0:
                            sp.wait_ge(k_scratch_in, nb.count(16 * PARTS, 16 * PARTS))
                        for r in range(PARTS):
                            sp.dma_start(k_op[ROT * r:ROT * (r + 1), heads, :],
                                         k_scratch[heads].rearrange("h i d n -> (i d) h n")).then_inc(qk_in[g], 16)

            run(sp, iteration)

        @block.tensor
        def _(pe):
            mm, transpose = nc.tensor.matmul, nc.tensor.transpose

            def next_fill(st, b, fill):
                back = 2 if alone(st, b) and fill in ("fc1.1", "fc1.2", "fc1.3", "fc2") else 1
                if b.any(len(st.fills), st.n(fill) - back + (st is post)):
                    pe.wait_ge(st.free, b.count(len(st.fills), st.n(fill) - back + (st is post)))

            def transposes(st, b, fill, rows):
                for t in range(TT):
                    last = transpose(st.bank[:, P * t:P * (t + 1)], rows[:, t, :], ident[:, :])
                last.then_inc(st.full, 1)

            def three_products(bank, w_hi, w_lo, m_hi, m_lo, start, stop, low_in, low_count):
                mm(bank, w_hi, m_hi, start=start, stop=False)
                mm(bank, w_lo, m_hi, start=False, stop=False)
                pe.wait_ge(low_in, low_count)
                return mm(bank, w_hi, m_lo, start=False, stop=stop)

            def ffn(st, b, per_lo, what):
                if what == "hT":
                    pe.wait_ge(st.rows, b.count(per_lo, 1))
                    next_fill(st, b, "hT")
                    transposes(st, b, "hT", st.h)
                elif what.startswith("fc1"):
                    f = int(what[-1])
                    if st is pre and b.least == 0:
                        pe.wait_ge(w1_ready, 1)
                    next_fill(st, b, what)
                    cols = slice(P * f, P * (f + 1))
                    three_products(fc1_bank(st, b, f)[:, :], w1_hi[:, cols], w1_lo[:, cols], st.t_hi[:, :], st.t_lo[:, :],
                                   True, True, st.t_lo_in, b.count(per_lo, 1)
                                   ).then_inc(st.full, 1)
                elif what.startswith("fc2"):
                    f = int(what[-1])
                    if st is pre and b.least == 0:
                        pe.wait_ge(w2_ready, 1)
                    if f == 0:
                        next_fill(st, b, "fc2")
                    pe.wait_ge(st.y_hi_in, b.count(FT, f + 1))
                    last = three_products(st.bank[:, :], w2_hi[:, f, :], w2_lo[:, f, :],
                                          st.y_hi[:, f, :], st.y_lo[:, f, :], f == 0, f == FT - 1,
                                          st.y_lo_in, b.count(FT, f + 1))
                    if f == FT - 1:
                        last.then_inc(st.full, 1)
                elif what == "zT":
                    next_fill(st, b, "zT")
                    for t in range(TT):
                        last = transpose(st.bank[:, P * t:P * (t + 1)], st.z[:, P * t:P * (t + 1)], ident[:, :])
                    last.then_inc(st.full, 1)

            def step_scores(b, s):
                g, kt = divmod(s, TT)
                if kt == 0:
                    pe.wait_ge(qk_in[g], b.count(16 * QK_DMAS, 16 * QK_DMAS))
                for i in range(2):
                    for j in range(2):
                        if b.any(STEPS, s):
                            pe.wait_ge(probs_done[i], b.count(2 * STEPS, 2 * s - 1 + j))
                        h = heads_of(g).start + 2 * (2 * i + j)
                        mm(scores[i][:, j, :], k_op[:, h, P * kt:P * (kt + 1)], q_op[:, h, :],
                           start=True, stop=True).then_inc(scores_done[i], 1)

            def step_values(b, s):
                g, kt = divmod(s, TT)
                pair, odd = divmod(g, 2)
                if kt == 0:
                    pe.wait_ge(v_in, b.count(NG, g + 1))
                    if not odd and b.any(NP, pair - 1):
                        pe.wait_ge(a_done, b.count(NP, pair - 1))
                for i in range(2):
                    pe.wait_ge(probs_done[i], b.count(2 * STEPS, 2 * s + 2))
                for j in range(HG):
                    last = mm(o_bank[pair][VW * j:VW * (j + 1), :], v_op[:, kt, heads_of(g).start + 2 * j, :],
                              probs[:, s % 2, j, :], start=(odd == 0 and kt == 0), stop=(odd == 1 and kt == TT - 1))
                last.then_inc(pv_done, 1)

            def task(stage, what, b):
                if stage == "oT":
                    pair = int(what)
                    pe.wait_ge(o_out, b.count(NP, pair + 1))
                    for t in range(TT):
                        last = transpose(o_bank[pair][:, P * t:P * (t + 1)],
                                         o_sums[:, pair, P * t:P * (t + 1)], ident[:, :])
                    last.then_inc(oT_done, 1)
                elif stage == "pre":
                    if what == "uT":
                        pe.wait_ge(pre.rows, b.count(2, 2))
                        next_fill(pre, b, "uT")
                        transposes(pre, b, "uT", u1)
                    elif what in ("q", "k"):
                        i = "qk".index(what)
                        if b.least == 0:
                            pe.wait_ge(wqkv_ready, 1)
                        next_fill(pre, b, what)
                        three_products(pre.bank[:, :], wqk_hi[:, i, :], wqk_lo[:, i, :], pre.t_hi[:, :],
                                       pre.t_lo[:, :], True, True, pre.t_lo_in, b.count(2, 2)
                                       ).then_inc(pre.full, 1)
                    elif what == "v":
                        next_fill(pre, b, "v")
                        for t in range(TT):
                            last = mm(pre.bank[:, P * t:P * (t + 1)], pre.t[:, P * t:P * (t + 1)], wv[:, :],
                                      start=True, stop=True)
                        last.then_inc(pre.full, 1)
                    else:
                        ffn(pre, b, 2, what)
                elif stage == "post":
                    if what == "aT":
                        pe.wait_ge(a_done, b.count(NP, NP))
                        next_fill(post, b, "aT")
                        for t in range(TT):
                            last = transpose(post.bank[:, P * t:P * (t + 1)],
                                             a_rows[:, t, :, :].rearrange("p h d -> p (h d)"), ident[:, :])
                        last.then_inc(post.full, 1)
                    elif what == "op":
                        if b.least == 0:
                            pe.wait_ge(wo_loaded, 16)
                        next_fill(post, b, "op")
                        for t in range(TT):
                            last = mm(post.bank[:, P * t:P * (t + 1)], aT[:, P * t:P * (t + 1)], wo[:, :],
                                      start=True, stop=True)
                        last.then_inc(post.full, 1)
                    else:
                        ffn(post, b, 1, what)

            def iteration(b):
                for s, (early, late) in enumerate(SCHEDULE):
                    if b.exists():
                        step_scores(b, s)
                    for stage, what, tb in tasks(b, early):
                        task(stage, what, tb)
                    if s == 0 and (b + (-1)).exists():
                        step_values(b + (-1), STEPS - 1)
                    elif s > 0 and b.exists():
                        step_values(b, s - 1)
                    for stage, what, tb in tasks(b, late):
                        task(stage, what, tb)

            pe.wait_ge(pool_ready, 1)
            run(pe, iteration)

        @block.scalar
        def _(act):
            activation = nc.scalar.activation
            act.dma_start(pre.x[:, :, :], x_rows[0]).then_inc(x_loaded, 16)
            for dst, src, loaded in (
                (g_col[:, :], ln_gamma.unsqueeze(1), columns_loaded), (be_col[:, :], ln_beta.unsqueeze(1), columns_loaded),
                (b1_col[:, :], fc1_bias.rearrange("(p f) -> p f", f=FT), columns_loaded),
                (b2_col[:, :], fc2_bias.unsqueeze(1), b2_loaded),
                (gamma_rows[:, :], gamma.unsqueeze(0).to_broadcast([P, D]), rows_loaded),
                (beta_rows[:, :], beta.unsqueeze(0).to_broadcast([P, D]), rows_loaded),
                (bo_rows[:, :], b_out.unsqueeze(0).to_broadcast([P, D]), rows_loaded),
            ):
                act.dma_start(dst, src).then_inc(loaded, 16)

            def ffn(st, b, what):
                n, per = st.n("fc2" if what == "fc2.3" else what), len(st.fills)
                if what == "hT":
                    act.wait_ge(st.full, b.count(per, n))
                    activation(st.t[:, :], st.bank[:, :], ACT.Identity, bias=be_col[:, :], scale=g_col[:, :])
                    activation(st.t_hi[:, :], st.bank[:, :], ACT.Identity, bias=be_col[:, :], scale=g_col[:, :]
                               ).then_inc(st.free, 1)
                elif what.startswith("fc1"):
                    f = int(what[-1])
                    act.wait_ge(st.full, b.count(per, n))
                    if f >= 2:
                        act.wait_ge(st.y_lo_in, b.count(FT, f - 1))
                    activation(st.y[:, f % 2, :], fc1_bank(st, b, f)[:, :], ACT.Silu, bias=b1_col[:, f:f + 1]
                               ).then_inc(st.free, 1)
                elif what == "fc2.3":
                    if st is pre and b.least == 0:
                        act.wait_ge(w2_ready, 1)
                    act.wait_ge(st.full, b.count(per, n))
                    activation(st.z[:, :], st.bank[:, :], ACT.Identity, bias=b2_quarter[:, :], scale=0.25
                               ).then_inc(st.free, 1)

            def residual(st, b):
                act.wait_ge(st.mixed, b.count(1, 1))
                if st is post and b.any(len(st.fills), 1):
                    act.wait_ge(st.free, b.count(len(st.fills), 1))
                for t in range(TT):
                    last = activation(st.xr[:, t, :], st.x[:, t, :], ACT.Identity, bias=st.mix[:, 1, t:t + 1],
                                      scale=st.mix[:, 0, t:t + 1])
                last.then_inc(st.res, 1)

            def task(stage, what, b):
                if stage == "o_out":
                    pair = int(what)
                    act.wait_ge(pv_done, b.count(STEPS, 2 * TT * (pair + 1)))
                    if b.any(NP, pair - 1):
                        act.wait_ge(oT_done, b.count(NP, pair - 1))
                    activation(o_sums[:, pair, :], o_bank[pair][:, :], ACT.Copy).then_inc(o_out, 1)
                elif stage == "pre":
                    per = len(PRE_FILLS)
                    if what == "uT":
                        act.wait_ge(pre.full, b.count(per, pre.n("uT")))
                        activation(pre.t[:, :], pre.bank[:, :], ACT.Copy)
                        activation(pre.t_hi[:, :], pre.bank[:, :], ACT.Copy).then_inc(pre.free, 1)
                    elif what in ("q", "k"):
                        i, scale = "qk".index(what), (HD ** -0.5 if what == "q" else 1.0)
                        if b.any(16, 0):
                            if i == 0:
                                act.wait_ge(q_scratch_in, b.count(16 * Q_DMAS, 0))
                            else:
                                act.wait_ge(k_scratch_in, b.count(16 * PARTS, 0))
                        act.wait_ge(pre.full, b.count(per, pre.n(what)))
                        activation(qk[:, i, :], pre.bank[:, :], ACT.Copy, scale=scale).then_inc(pre.free, 1)
                        act.wait_ge(pre.free, b.count(per, pre.n(what)))
                        activation(qk_parts[:, i, 0, :], qk[:, i, :], ACT.Copy).then_inc(high_in[i], 1)
                    elif what == "v":
                        if b.any(NG, 0):
                            act.wait_ge(v_in, b.count(NG, 0))
                        act.wait_ge(pre.full, b.count(per, pre.n("v")))
                        activation(v_rows[:, :, :], pre.bank[:, :].rearrange("p (t d) -> p t d", t=TT), ACT.Copy
                                   ).then_inc(pre.free, 1)
                    elif what == "xr":
                        residual(pre, b)
                    elif what == "load_x" and b.least > 0:
                        load_x(b)
                    elif what in pre.fills or what == "fc2.3":
                        ffn(pre, b, what)
                elif stage == "post":
                    if what == "aT":
                        act.wait_ge(post.full, b.count(len(POST_FILLS), post.n("aT")))
                        activation(aT[:, :], post.bank[:, :], ACT.Copy).then_inc(post.free, 1)
                    elif what == "xr":
                        residual(post, b)
                    elif what == "x_apply":
                        act.wait_ge(post.centred, b.count(1, 1))
                        for t in range(TT):
                            last = activation(post.h[:, t, :], post.x[:, t, :], ACT.Identity,
                                              bias=post.minus_mr[:, t:t + 1], scale=post.rs[:, 1, t:t + 1])
                        last.then_inc(post.rows, 1)
                    elif what in post.fills or what == "fc2.3":
                        ffn(post, b, what)
                elif stage == "carry":
                    act.wait_ge(held, b.count(1, 1))
                    if b.any(1, 0):
                        act.wait_ge(x2_done, b.count(1, 0))
                    activation(x1_beta[:, :, :], x1_held[:, :, :], ACT.Copy).then_inc(carried, 1)

            def load_x(b):
                if b.any(1, 0):
                    act.wait_ge(pre.res, b.count(1, 0))
                act.dma_start(pre.x[:, :, :], x_rows[b.index]).then_inc(x_loaded, 16)

            def store_out(b):
                act.wait_ge(post.free, b.count(len(POST_FILLS), post.n("zT") + 1))
                act.dma_start(out_rows[b.index], o_rows[:, :, :]).then_inc(out_stored, 16)

            def iteration(b):
                for s, (early, late) in enumerate(SCHEDULE):
                    if b.exists():
                        if b.any(STEPS, s - 1):
                            act.wait_ge(pv_done, b.count(STEPS, s - 1))
                        for j in range(2):
                            act.wait_ge(scores_done[0], b.count(2 * STEPS, 2 * s + j + 1))
                            activation(probs[:, s % 2, j, :], scores[0][:, j, :], ACT.Relu).then_inc(probs_done[0], 1)
                    for stage, what, tb in tasks(b, early + late):
                        task(stage, what, tb)
                if (b + (-1)).exists():
                    store_out(b + (-1))

            act.wait_ge(ident_zero, 1)
            activation(post.tmp[:, :], ones[:, 0:1], ACT.Silu)
            act.wait_ge(columns_loaded, 48)
            run(act, iteration)
            act.wait_ge(out_stored, 16 * (B + 1))

        @block.vector
        def _(dve):
            v = nc.vector
            PRE_LINKS, POST_LINKS, SPLIT_LINKS, NORM_LINKS = 4, 5, 4, 2 * NP

            def prepare_w(k, w_int, w_loaded, w_raw, scales, w_hi, w_lo, ready):
                dve.wait_ge(w_loaded, 32)
                v.tensor_copy(w_raw, w_int).then_inc(w_link, 1)
                dve.wait_ge(w_link, k + 1)
                v.scalar_tensor_tensor(w_raw, w_raw, -ZERO_POINT, scales, ALU.add, ALU.mult).then_inc(w_link, 1)
                dve.wait_ge(w_link, k + 2)
                v.tensor_copy(w_hi, w_raw).then_inc(w_link, 1)
                dve.wait_ge(w_link, k + 3)
                v.tensor_tensor(w_lo, w_raw, w_hi.bitcast(F32), ALU.subtract).then_inc(ready, 1)

            def prepare_qkv():
                dve.wait_ge(wqkv_loaded, 16)
                raw = w_raw[:, :].rearrange("p (h c d) -> p c h d", c=3, d=HD)
                for i in range(2):
                    v.tensor_copy(wqk[:, i, :].rearrange("p (h d) -> p h d", d=HD), raw[:, i])
                v.tensor_copy(wv[:, :].rearrange("p (h d) -> p h d", d=HD), raw[:, 2]).then_inc(w_link, 1)
                dve.wait_ge(w_link, 7)
                v.tensor_copy(wqk_hi[:, :, :], wqk[:, :, :]).then_inc(w_link, 1)
                dve.wait_ge(w_link, 8)
                v.tensor_tensor(wqk_lo[:, :, :], wqk[:, :, :], wqk_hi[:, :, :].bitcast(F32), ALU.subtract
                                ).then_inc(wqkv_ready, 1)

            def prepare(b, what):
                if b.least == -2 and what == "x_apply":
                    prepare_w(0, w1_int[:, :], w1_loaded, w1_raw[:, :], s1_rows[:, :], w1_hi[:, :], w1_lo[:, :], w1_ready)
                elif b.least == -2 and what == "high.0":
                    dve.wait_ge(b2_loaded, 16)
                    v.tensor_scalar(b2_quarter[:, :], b2_col[:, :], 0.25, None, ALU.mult)
                    prepare_w(3, w2_int[:, :, :], w2_loaded, w2_raw[:, :, :], s2_rows[:, :, :],
                              w2_hi[:, :, :], w2_lo[:, :, :], w2_ready)
                elif b.least == -1 and what == "high.3":
                    prepare_qkv()
                    v.memset(q_op[64:QK_ROWS, :, :].bitcast(F32), 0.0)
                elif b.least == -1 and what == "u_apply":
                    v.memset(k_op[64:QK_ROWS, :, :].bitcast(F32), 0.0).then_inc(zero_rows, 1)

            def row_stats(st, b, per, k, rows, n):
                for t in range(TT):
                    last = v.bn_stats(st.stats[:, t, :], rows[:, t, :])
                last.then_inc(st.dve_link, 1)
                dve.wait_ge(st.dve_link, b.count(per, k + 1))
                v.tensor_copy(st.tmp[:, 0:1], st.stats[:, 0, 0:1])
                for t in range(TT):
                    last = v.bn_aggr(st.mv[:, t, :], st.stats[:, t, :])
                last.then_inc(st.dve_link, 1)
                dve.wait_ge(st.dve_link, b.count(per, k + 2))
                v.tensor_scalar(st.minus_mean[:, :], st.mv[:, :, 0], -1.0, None, ALU.mult)
                var = st.mv[:, :, 1]
                last = v.tensor_scalar(st.var[:, 0, :], var, LN_EPS, None, ALU.add)
                if n == 2:
                    last = v.tensor_scalar(st.var[:, 1, :], var, 1.0 + LN_EPS, LN_EPS ** 2, ALU.mult, ALU.add)
                last.then_inc(st.var_in, 1)

            def normalise(st, dst, rows, i):
                for t in range(TT):
                    last = v.tensor_scalar(dst[:, t, :], rows[:, t, :], st.mv[:, t, 0:1], st.rs[:, i, t:t + 1],
                                           ALU.subtract, ALU.mult)
                return last

            def high_y(st, b, f):
                dve.wait_ge(st.free, b.count(len(st.fills), st.n(f"fc1.{f}") + (st is post)))
                v.tensor_copy(st.y_hi[:, f, :], st.y[:, f % 2, :]).then_inc(st.y_hi_in, 1)

            def task(stage, what, b):
                if what.startswith("high"):
                    high_y({"pre": pre, "post": post}[stage], b, int(what[-1]))
                elif stage == "oT":
                    pair = int(what)
                    if pair == 0:
                        if (b + (-1)).any(len(POST_FILLS), post.n("aT")):
                            dve.wait_ge(post.full, (b + (-1)).count(len(POST_FILLS), post.n("aT")))
                    dve.wait_ge(oT_done, b.count(NP, pair + 1))
                    sums = o_bank[pair][:, :].rearrange("p (t h c) -> p t h c", t=TT, c=HW)
                    v.tensor_scalar(den[:, :, :], sums[:, :, :, HD], KERN_EPS, None, ALU.add).then_inc(norm_link, 1)
                    dve.wait_ge(norm_link, b.count(NORM_LINKS, 2 * pair + 1))
                    v.reciprocal(rec[:, :, :], den[:, :, :]).then_inc(norm_link, 1)
                    dve.wait_ge(norm_link, b.count(NORM_LINKS, 2 * pair + 2))
                    v.tensor_tensor(a_rows[:, :, PH * pair:PH * (pair + 1), :], sums[:, :, :, 0:HD],
                                    rec[:, :, :].unsqueeze(3).to_broadcast([P, TT, PH, HD]), ALU.mult
                                    ).then_inc(a_done, 1)
                elif stage == "pre":
                    per = len(PRE_FILLS)
                    if what == "x_stats":
                        dve.wait_ge(x_loaded, b.count(16, 16))
                        row_stats(pre, b, PRE_LINKS, 0, pre.x, 2)
                    elif what == "x_apply":
                        dve.wait_ge(pre.rsqrt, b.count(2, 1))
                        normalise(pre, pre.h, pre.x, 1).then_inc(pre.rows, 1)
                    elif what == "x1":
                        dve.wait_ge(pre.full, b.count(per, pre.n("zT")))
                        dve.wait_ge(pre.res, b.count(1, 1))
                        if b.any(1, 0):
                            dve.wait_ge(held, b.count(1, 0))
                        v.tensor_tensor(x1[:, :, :], pre.bank[:, :].rearrange("p (t d) -> p t d", t=TT),
                                        pre.xr[:, :, :], ALU.add).then_inc(pre.free, 1)
                    elif what == "x1_stats":
                        dve.wait_ge(pre.free, b.count(per, pre.n("zT")))
                        row_stats(pre, b, PRE_LINKS, 2, x1, 1)
                    elif what == "u_apply":
                        dve.wait_ge(pre.rsqrt, b.count(2, 2))
                        if b.any(1, 0):
                            dve.wait_ge(u_carried, b.count(1, 0))
                        normalise(pre, u1, x1, 0).then_inc(pre.rows, 1)
                    elif what in ("split_q", "split_k"):
                        i = ("split_q", "split_k").index(what)
                        dve.wait_ge(high_in[i], b.count(1, 1))
                        v.tensor_tensor(qk[:, i, :], qk[:, i, :], qk_parts[:, i, 0, :], ALU.subtract
                                        ).then_inc(split_link, 1)
                        dve.wait_ge(split_link, b.count(SPLIT_LINKS, 2 * i + 1))
                        v.tensor_copy(qk_parts[:, i, 1, :], qk[:, i, :]).then_inc(split_link, 1)
                        dve.wait_ge(split_link, b.count(SPLIT_LINKS, 2 * i + 2))
                        v.tensor_tensor(qk_parts[:, i, 2, :], qk[:, i, :], qk_parts[:, i, 1, :], ALU.subtract
                                        ).then_inc(parts_ready[i], 1)
                elif stage == "post":
                    per = len(POST_FILLS)
                    if what == "y":
                        dve.wait_ge(post.full, b.count(per, post.n("op")))
                        dve.wait_ge(u_carried, b.count(1, 1))
                        v.tensor_tensor(y_rows[:, :, :], post.bank[:, :].rearrange("p (t d) -> p t d", t=TT),
                                        u1_bias[:, :, :], ALU.add).then_inc(post.free, 1)
                    elif what == "y_stats":
                        dve.wait_ge(post.free, b.count(per, post.n("op") + 1))
                        row_stats(post, b, POST_LINKS, 0, y_rows, 1)
                    elif what == "y_gamma":
                        dve.wait_ge(post.var_in, b.count(2, 1))
                        for t in range(TT):
                            last = v.scalar_tensor_tensor(y_rows[:, t, :], y_rows[:, t, :], post.mv[:, t, 0:1],
                                                          gamma_rows[:, :], ALU.subtract, ALU.mult)
                        last.then_inc(post.dve_link, 1)
                    elif what == "x2":
                        dve.wait_ge(post.rsqrt, b.count(2, 1))
                        dve.wait_ge(carried, b.count(1, 1))
                        dve.wait_ge(post.dve_link, b.count(POST_LINKS, 3))
                        for t in range(TT):
                            last = v.scalar_tensor_tensor(post.x[:, t, :], y_rows[:, t, :], post.rs[:, 0, t:t + 1],
                                                          x1_beta[:, t, :], ALU.mult, ALU.add)
                        last.then_inc(x2_done, 1)
                    elif what == "x2_stats":
                        dve.wait_ge(x2_done, b.count(1, 1))
                        row_stats(post, b, POST_LINKS, 3, post.x, 2)
                    elif what == "zT":
                        dve.wait_ge(post.full, b.count(per, post.n("zT")))
                        dve.wait_ge(post.res, b.count(1, 1))
                        dve.wait_ge(out_stored, b.count(16, 16))
                        v.tensor_tensor(o_rows[:, :, :], post.bank[:, :].rearrange("p (t d) -> p t d", t=TT),
                                        post.xr[:, :, :], ALU.add).then_inc(post.free, 1)

            def iteration(b):
                for s, (early, late) in enumerate(SCHEDULE):
                    if b.exists():
                        if b.any(STEPS, s - 1):
                            dve.wait_ge(pv_done, b.count(STEPS, s - 1))
                        for j in range(2):
                            dve.wait_ge(scores_done[1], b.count(2 * STEPS, 2 * s + j + 1))
                            v.tensor_scalar(probs[:, s % 2, 2 + j, :], scores[1][:, j, :], 0.0, None, ALU.max
                                            ).then_inc(probs_done[1], 1)
                    for stage, what, tb in tasks(b, early + late):
                        task(stage, what, tb)
                        prepare(b, what)

            v.memset(rec[:, 0, 0:1], 0.0).then_inc(post.free, 1)
            v.memset(den[:, 0, 0:1], 0.0).then_inc(out_stored, 16)
            run(dve, iteration)

        @block.gpsimd
        def _(pool):
            p = nc.gpsimd
            p.memset(minus_half[:, :], -0.5)
            p.memset(half[:, :], 0.5)
            p.memset(ones[:, :], 1.0).then_inc(ident_zero, 1)
            p.memset(ident[:, :], 0.0).then_inc(ident_zero, 1)
            pool.wait_ge(ident_zero, 2)
            p.affine_select(out=ident[:, :], in_=ident[:, :], compare_op=ALU.not_equal, fill=1.0, base=0,
                            pattern=[[-1, P]], channel_multiplier=1).then_inc(pool_ready, 1)
            p.memset(v_op[:, :, :, :], 0.0).then_inc(v_ready, 1)
            pool.wait_ge(v_ready, 1)
            for odd in range(2):
                p.memset(v_op[:, :, odd::2, HW * odd + HD:HW * odd + HD + 1], 1.0).then_inc(v_ready, 1)

            def deviations(st, b, k, n, centred):
                pool.wait_ge(st.var_in, b.count(2, k))
                i = n - 1
                p.tensor_tensor(st.rs[:, i, :], st.var[:, i, :], minus_half[:, :], ALU.pow).then_inc(st.rsqrt, 1)
                pool.wait_ge(st.rsqrt, b.count(2, k))
                if centred:
                    p.tensor_tensor(st.minus_mr[:, :], st.minus_mean[:, :], st.rs[:, i, :], ALU.mult
                                    ).then_inc(st.centred, 1)
                if n == 2:
                    p.tensor_tensor(st.rs[:, 0, :], st.var[:, 0, :], minus_half[:, :], ALU.pow).then_inc(st.pool_link, 1)
                    pool.wait_ge(st.pool_link, b.count(2, 1))
                    p.tensor_tensor(st.half_r[:, :], st.rs[:, 0, :], half[:, :], ALU.mult).then_inc(st.pool_link, 1)
                    pool.wait_ge(st.pool_link, b.count(2, 2))
                    if b.any(1, 0):
                        pool.wait_ge(st.res, b.count(1, 0))
                    p.tensor_tensor(st.mix[:, 0, :], ones[:, :], st.half_r[:, :], ALU.add)
                    p.tensor_tensor(st.mix[:, 1, :], st.minus_mean[:, :], st.half_r[:, :], ALU.mult
                                    ).then_inc(st.mixed, 1)

            def low_t(st, b, fill):
                pool.wait_ge(st.free, b.count(len(st.fills), st.n(fill) + (st is post)))
                p.tensor_tensor(st.t_lo[:, :], st.t[:, :], st.t_hi[:, :].bitcast(F32), ALU.subtract
                                ).then_inc(st.t_lo_in, 1)

            def low_y(st, b, f):
                pool.wait_ge(st.y_hi_in, b.count(FT, f + 1))
                p.tensor_tensor(st.y_lo[:, f, :], st.y[:, f % 2, :], st.y_hi[:, f, :].bitcast(F32), ALU.subtract
                                ).then_inc(st.y_lo_in, 1)

            def task(stage, what, b):
                if stage == "v_in":
                    g = int(what)
                    if b.least == 0:
                        pool.wait_ge(v_ready, 3)
                    pool.wait_ge(pre.free, b.count(len(PRE_FILLS), pre.n("v")))
                    if (b + (-1)).any(STEPS, TT * (g + 1)):
                        pool.wait_ge(pv_done, (b + (-1)).count(STEPS, TT * (g + 1)))
                    heads, first = heads_of(g), HW * (g % 2)
                    rows = v_rows[:, :, :].rearrange("p t (h d) -> p t h d", d=HD)[:, :, heads, :]
                    by_one = v_op[:, :, heads, first + HD:first + HD + 1].to_broadcast([P, TT, HG, HD])
                    p.tensor_tensor(v_op[:, :, heads, first:first + HD], rows, by_one, ALU.mult).then_inc(v_in, 1)
                elif stage == "hold":
                    pool.wait_ge(pre.rows, b.count(2, 2))
                    if b.least == 0:
                        pool.wait_ge(rows_loaded, 48)
                    if b.any(1, 0):
                        pool.wait_ge(carried, b.count(1, 0))
                    p.tensor_tensor(x1_held[:, :, :], x1[:, :, :], beta_rows[:, :].unsqueeze(1).to_broadcast([P, TT, D]),
                                    ALU.add).then_inc(held, 1)
                elif stage == "carry_u":
                    last_batch, per = b + (-1), len(POST_FILLS)
                    if last_batch.any(per, post.n("op") + 1):
                        pool.wait_ge(post.free, last_batch.count(per, post.n("op") + 1))
                    p.tensor_tensor(u1_bias[:, :, :], u1[:, :, :], bo_rows[:, :].unsqueeze(1).to_broadcast([P, TT, D]),
                                    ALU.add).then_inc(u_carried, 1)
                elif stage == "pre":
                    if what == "x_stats":
                        deviations(pre, b, 1, 2, centred=False)
                    elif what in ("hT", "uT"):
                        low_t(pre, b, what)
                    elif what.startswith("low"):
                        low_y(pre, b, int(what[-1]))
                    elif what == "x1_stats":
                        deviations(pre, b, 2, 1, centred=False)
                elif stage == "post":
                    if what == "y_stats":
                        deviations(post, b, 1, 1, centred=False)
                    elif what == "x2_stats":
                        deviations(post, b, 2, 2, centred=True)
                    elif what == "hT":
                        low_t(post, b, what)
                    elif what.startswith("low"):
                        low_y(post, b, int(what[-1]))

            def iteration(b):
                for early, late in SCHEDULE:
                    for stage, what, tb in tasks(b, early + late):
                        task(stage, what, tb)

            run(pool, iteration)


_INS = ['L0_attn_x', 'L0_attn_w_qkv', 'L0_attn_w_out', 'L0_attn_b_out', 'L0_attn_gamma', 'L0_attn_beta',
        'L0_ffn_ln_gamma', 'L0_ffn_ln_beta', 'L0_ffn_fc1_q', 'L0_ffn_fc1_scales', 'L0_ffn_fc1_bias',
        'L0_ffn_fc2_q', 'L0_ffn_fc2_scales', 'L0_ffn_fc2_bias']


def kernel(**inputs):
    import numpy as _np
    import concourse.bacc as _bacc
    from concourse import mybir as _mybir
    from concourse.bass_utils import run_bass_kernel_spmd as _run

    nc = _bacc.Bacc("TRN2", target_bir_lowering=False, num_devices=1)
    arrays, args = {}, []
    for name in _INS:
        a = _np.ascontiguousarray(inputs[name])
        if name == 'L0_ffn_fc1_bias':
            a = _np.ascontiguousarray(a.reshape(FT, P).T).reshape(-1)
        arrays[f"in_{name}_dram"] = a
        args.append(nc.dram_tensor(f"in_{name}_dram", a.shape, _mybir.dt.from_np(a.dtype), kind="ExternalInput").ap())
    out = nc.dram_tensor("out_0_dram", (B, S, D), F32, kind="ExternalOutput").ap()
    build(nc, *args, out)
    r = _run(nc, [arrays], core_ids=[0])
    return r.results[0]["out_0_dram"]
```
